# Optimizing a Trainium2 kernel written in Bass

```python
import numpy as np
import jax
import jax.numpy as jnp

def _softmax(x, axis=-1):
    return jax.nn.softmax(x, axis=axis)

def _gelu(x):
    return jax.nn.gelu(x, approximate=True)

def _silu(x):
    return jax.nn.silu(x)

def _sigmoid(x):
    return jax.nn.sigmoid(x)

def _layernorm(x, axis=-1, eps=1e-05):
    m = jnp.mean(x, axis=axis, keepdims=True)
    v = jnp.var(x, axis=axis, keepdims=True)
    return (x - m) / jnp.sqrt(v + eps)

def _scatter_add(tgt, idx, src, axis=0):
    return tgt.at[idx].add(src)

def _segment_sum(src, seg, n):
    return jax.ops.segment_sum(src, seg, n)
kernel_name = 'mk_adj_resnorm_d4_adj_r2_eee89a'

def setup_inputs(seed: int=0):
    np.random.seed(seed)
    _w = jnp.asarray

    def _rec_inputs():
        import jax
        import jax.numpy as jnp
        _gk = jax.random.key(seed)
        x = -0.0002928 + 1 * jax.random.normal(jax.random.fold_in(_gk, 1), (16, 512, 128), jnp.float32)
        _a = jax.random.bernoulli(jax.random.fold_in(_gk, 2), 0.00390625, (512, 512))
        _a = jnp.logical_or(_a, jnp.swapaxes(_a, -1, -2))
        _a = jnp.logical_or(_a, jnp.eye(512, dtype=bool))
        _af = _a.astype(jnp.float32)
        _af = _af * jax.random.uniform(jax.random.fold_in(_gk, 3), (512, 512), jnp.float32, 0.05, 1)
        adj = _af
        return (x, adj)
    x, adj = _rec_inputs()

    def _L0_gnn_setup():
        import jax, jax.numpy as jnp
        import numpy as np
        B, N, D = (32, 512, 128)
        TIME_STEP = 5
        key = jax.random.key(seed)
        ks = jax.random.split(key, 12)
        s2 = 1.0 / np.sqrt(2 * D)
        s1 = 1.0 / np.sqrt(D)
        return {'input': jax.random.normal(ks[0], (B, N, D), jnp.float32), 'in_matrix': jax.random.uniform(ks[1], (N, N), jnp.float32), 'out_matrix': jax.random.uniform(ks[2], (N, N), jnp.float32), 'w3_w': jax.random.normal(ks[3], (D, 2 * D), jnp.float32) * s2, 'w3_b': jnp.zeros((D,), jnp.float32), 'u3_w': jax.random.normal(ks[4], (D, D), jnp.float32) * s1, 'u3_b': jnp.zeros((D,), jnp.float32), 'w4_w': jax.random.normal(ks[5], (D, 2 * D), jnp.float32) * s2, 'w4_b': jnp.zeros((D,), jnp.float32), 'w5_w': jax.random.normal(ks[6], (D, 2 * D), jnp.float32) * s2, 'w5_b': jnp.zeros((D,), jnp.float32), 'u5_w': jax.random.normal(ks[7], (D, D), jnp.float32) * s1, 'u5_b': jnp.zeros((D,), jnp.float32), 'time_step': TIME_STEP}
    _L0_gnn_all = _L0_gnn_setup()
    _L0_gnn_in = {k: v for k, v in _L0_gnn_all.items() if k in ('w3_w', 'w3_b', 'u3_w', 'u3_b', 'w4_w', 'w4_b', 'w5_w', 'w5_b', 'u5_w', 'u5_b')}
    del _L0_gnn_all

    def _L1_gnn_setup():
        import jax, jax.numpy as jnp
        import numpy as np
        _NEG_INF = -1000000000.0
        ALPHA = 0.2
        key = jax.random.key(seed)
        k0, k1, k2, k3, k4 = jax.random.split(key, 5)
        B, N, F_IN, F_OUT = (8, 1024, 128, 128)
        x = jax.random.normal(k0, (B, N, F_IN), dtype=jnp.float32)
        adj = (jax.random.uniform(k1, (N, N)) < 0.02).astype(jnp.float32)
        W = jax.random.normal(k2, (F_IN, F_OUT), dtype=jnp.float32) * (1.0 / np.sqrt(F_IN))
        bound = float(np.sqrt(6.0 / (F_OUT + 1)))
        a_src = jax.random.uniform(k3, (F_OUT, 1), minval=-bound, maxval=bound, dtype=jnp.float32)
        a_dst = jax.random.uniform(k4, (F_OUT, 1), minval=-bound, maxval=bound, dtype=jnp.float32)
        return {'x': x, 'adj': adj, 'W': W, 'a_src': a_src, 'a_dst': a_dst}
    _L1_gnn_all = _L1_gnn_setup()
    _L1_gnn_in = {k: v for k, v in _L1_gnn_all.items() if k in ('W', 'a_src', 'a_dst')}
    del _L1_gnn_all

    def _L2_gnn_setup():
        import jax, jax.numpy as jnp
        import numpy as np
        from jax import lax
        CONV_ORDER = 3

        def _chebyshev(adj, x, order):

            def step(carry, _):
                nxt = jnp.einsum('ij,bjc->bic', adj, carry)
                return (nxt, nxt)
            _, xs = lax.scan(step, x, None, length=order)
            return jnp.moveaxis(xs, 0, -1)
        key = jax.random.key(seed)
        k1, k2, k3, k4 = jax.random.split(key, 4)
        B, E, C_in, C_out, K, n_adjs = (8, 2048, 128, 128, CONV_ORDER, 2)
        x_1 = jax.random.normal(k1, (B, E, C_in), dtype=jnp.float32)
        adj0 = jax.random.normal(k2, (E, E), dtype=jnp.float32) / np.sqrt(E)
        adj1 = jax.random.normal(k3, (E, E), dtype=jnp.float32) / np.sqrt(E)
        kdim = K * n_adjs + 1
        std = 1.414 * np.sqrt(2.0 / float((C_in + C_out) * kdim))
        weight_1 = std * jax.random.normal(k4, (C_in, C_out, kdim), dtype=jnp.float32)
        return {'x_1': x_1, 'adj0': adj0, 'adj1': adj1, 'weight_1': weight_1}
    _L2_gnn_all = _L2_gnn_setup()
    _L2_gnn_in = {k: v for k, v in _L2_gnn_all.items() if k in ('weight_1',)}
    del _L2_gnn_all

    def _L3_gnn_setup():
        import jax, jax.numpy as jnp
        import numpy as np
        B, N, D = (32, 512, 128)
        LEAKY_ALPHA = 0.2
        LN_EPS = 1e-14
        key = jax.random.key(seed)
        k1, k2 = jax.random.split(key)
        x = jax.random.normal(k1, (B, N, D), dtype=jnp.float32)
        limit = 1.414 * np.sqrt(6.0 / (2 * D + 1))
        a = jax.random.uniform(k2, (2 * D, 1), dtype=jnp.float32, minval=-limit, maxval=limit)
        gamma = jnp.ones((N, N), dtype=jnp.float32)
        beta = jnp.zeros((N, N), dtype=jnp.float32)
        return {'x': x, 'a': a, 'gamma': gamma, 'beta': beta}
    _L3_gnn_all = _L3_gnn_setup()
    _L3_gnn_in = {k: v for k, v in _L3_gnn_all.items() if k in ('a',)}
    del _L3_gnn_all
    return {'x': x, 'adj': adj, 'L0_gnn_w3_w': _L0_gnn_in['w3_w'], 'L0_gnn_w3_b': _L0_gnn_in['w3_b'], 'L0_gnn_u3_w': _L0_gnn_in['u3_w'], 'L0_gnn_u3_b': _L0_gnn_in['u3_b'], 'L0_gnn_w4_w': _L0_gnn_in['w4_w'], 'L0_gnn_w4_b': _L0_gnn_in['w4_b'], 'L0_gnn_w5_w': _L0_gnn_in['w5_w'], 'L0_gnn_w5_b': _L0_gnn_in['w5_b'], 'L0_gnn_u5_w': _L0_gnn_in['u5_w'], 'L0_gnn_u5_b': _L0_gnn_in['u5_b'], 'L1_gnn_W': _L1_gnn_in['W'], 'L1_gnn_a_src': _L1_gnn_in['a_src'], 'L1_gnn_a_dst': _L1_gnn_in['a_dst'], 'L2_gnn_weight_1': _L2_gnn_in['weight_1'], 'L3_gnn_a': _L3_gnn_in['a']}

def reference(x, adj, L0_gnn_w3_w, L0_gnn_w3_b, L0_gnn_u3_w, L0_gnn_u3_b, L0_gnn_w4_w, L0_gnn_w4_b, L0_gnn_w5_w, L0_gnn_w5_b, L0_gnn_u5_w, L0_gnn_u5_b, L1_gnn_W, L1_gnn_a_src, L1_gnn_a_dst, L2_gnn_weight_1, L3_gnn_a):
    import jax
    import jax.numpy as jnp

    def _L0_gnn_ref(input, in_matrix, out_matrix, w3_w, w3_b, u3_w, u3_b, w4_w, w4_b, w5_w, w5_b, u5_w, u5_b, time_step):
        import jax, jax.numpy as jnp
        import numpy as np
        B, N, D = (32, 512, 128)
        TIME_STEP = 5

        def step(h, _):
            m_in = jnp.einsum('nm,bmd->bnd', in_matrix, h)
            m_out = jnp.einsum('nm,bmd->bnd', out_matrix, h)
            av = jnp.concatenate([m_in, m_out], axis=-1)
            u3 = h @ u3_w.T + u3_b
            z = jax.nn.sigmoid(av @ w3_w.T + w3_b + u3)
            r = jax.nn.sigmoid(av @ w4_w.T + w4_b + u3)
            hv = jnp.tanh(av @ w5_w.T + w5_b + (r * h @ u5_w.T + u5_b))
            h = (1.0 - z) * h + z * hv
            return (h, None)
        h, _ = jax.lax.scan(step, input, None, length=time_step)
        return h

    def _L1_gnn_ref(x, adj, W, a_src, a_dst):
        import jax, jax.numpy as jnp
        import numpy as np
        _NEG_INF = -1000000000.0
        ALPHA = 0.2
        h = jnp.einsum('bnf,fo->bno', x, W)
        N = h.shape[1]
        e_src = (h @ a_src)[..., 0]
        e_dst = (h @ a_dst)[..., 0]
        e = jax.nn.leaky_relu(e_src[:, :, None] + e_dst[:, None, :], negative_slope=ALPHA)
        adj_loops = jnp.clip(adj + jnp.eye(N, dtype=adj.dtype), 0.0, None)
        e = jnp.where(adj_loops[None, :, :] == 0, _NEG_INF, e)
        attn = jax.nn.softmax(e, axis=-1)
        attn = jnp.nan_to_num(attn, nan=0.0, posinf=0.0, neginf=0.0)
        h_prime = jnp.einsum('bij,bjo->bio', attn, h)
        return jax.nn.elu(h_prime)

    def _L2_gnn_ref(x_1, adj0, adj1, weight_1):
        import jax, jax.numpy as jnp
        import numpy as np
        from jax import lax
        CONV_ORDER = 3

        def _chebyshev(adj, x, order):

            def step(carry, _):
                nxt = jnp.einsum('ij,bjc->bic', adj, carry)
                return (nxt, nxt)
            _, xs = lax.scan(step, x, None, length=order)
            return jnp.moveaxis(xs, 0, -1)
        parts = [x_1[..., None], _chebyshev(adj0, x_1, CONV_ORDER), _chebyshev(adj1, x_1, CONV_ORDER)]
        x_all = jnp.concatenate(parts, axis=3)
        y_1 = jnp.einsum('bnik,iok->bno', x_all, weight_1)
        return y_1

    def _L3_gnn_ref(x, a, gamma, beta):
        import jax, jax.numpy as jnp
        import numpy as np
        B, N, D = (32, 512, 128)
        LEAKY_ALPHA = 0.2
        LN_EPS = 1e-14
        d = x.shape[-1]
        a_i = a[:d, 0]
        a_j = a[d:, 0]
        e = (x @ a_i)[:, :, None] + (x @ a_j)[:, None, :]
        mean = jnp.mean(e, axis=(1, 2), keepdims=True)
        var = jnp.mean(jnp.square(e - mean), axis=(1, 2), keepdims=True)
        e = (e - mean) * jax.lax.rsqrt(var + LN_EPS) * gamma + beta
        e = jnp.where(e >= 0, e, LEAKY_ALPHA * e)
        alpha = jax.nn.softmax(e, axis=1)
        h = jax.nn.sigmoid(jnp.einsum('bij,bjd->bid', alpha, x))
        return h
    x = _layernorm(x + _L0_gnn_ref(x, adj, adj, L0_gnn_w3_w, L0_gnn_w3_b, L0_gnn_u3_w, L0_gnn_u3_b, L0_gnn_w4_w, L0_gnn_w4_b, L0_gnn_w5_w, L0_gnn_w5_b, L0_gnn_u5_w, L0_gnn_u5_b, 5), axis=-1)
    x = _layernorm(x + _L1_gnn_ref(x, adj, L1_gnn_W, L1_gnn_a_src, L1_gnn_a_dst), axis=-1)
    x = _layernorm(x + _L2_gnn_ref(x, adj, adj, L2_gnn_weight_1), axis=-1)
    x = _layernorm(x + _L3_gnn_ref(x, L3_gnn_a, adj, adj), axis=-1)
    return x

_drawn_inputs = setup_inputs


def setup_inputs(seed=0):
    import zlib

    import numpy as np

    out = dict(_drawn_inputs(seed))
    spreads = {'L0_gnn_w3_b': (0.0, 0.1),
     'L0_gnn_u3_b': (0.0, 0.1),
     'L0_gnn_w4_b': (0.0, 0.8),
     'L0_gnn_w5_b': (0.0, 0.1),
     'L0_gnn_u5_b': (0.0, 0.1)}
    factors = {'L3_gnn_a': 8.0}
    for name, (base, spread) in spreads.items():
        noise = np.random.default_rng([zlib.crc32(name.encode()), seed]).standard_normal(out[name].shape)
        drawn = base * np.exp(spread * noise) if base else spread * noise
        out[name] = jnp.asarray(drawn.astype(out[name].dtype))
    for name, factor in factors.items():
        out[name] = (out[name] * factor).astype(out[name].dtype)
    return out
```

```python
from contextlib import ExitStack

import concourse.bass as bass
from concourse import mybir

F32 = mybir.dt.float32
F32R = mybir.dt.float32r
ALU = mybir.AluOpType
ACT = mybir.ActivationFunctionType

P = 128
LN_EPS = 1e-5
EDGE_EPS = 1e-14
SLOPE = 0.2
MASKED = -(2.0**100)

KEEP = dict(u3T=(0, 128), w_gat=(128, 256), ident=(256, 384), a_src=(384, 385), a_dst=(385, 386),
            a_i=(386, 387), a_j=(387, 388), w3_b=(388, 389), u3_b=(389, 390), w4_b=(390, 391),
            w5_b=(391, 392), u5_b=(392, 393), u5T=(393, 521))
TEMP = dict(w3T=(0, 256), w4T=(256, 512), w5T=(512, 768), cheb=(768, 1664), w_gatT=(1664, 1792))


def wait(eng, sem, value):
    if not (isinstance(value, int) and value <= 0):
        eng.wait_ge(sem, value)


class Chain:

    def __init__(self, eng, sem, per, at):
        self.eng, self.sem, self.per, self.at, self.n = eng, sem, per, at, 0

    def link(self, instruction):
        self.n += 1
        instruction.then_inc(self.sem, 1)
        self.eng.wait_ge(self.sem, self.at * self.per + self.n)

    def close(self):
        assert self.n == self.per


def build(nc, x_nat, x_tr, adj_nat, adj_tr, keep_pack, temp_pack, out):
    _, B, NT, D = x_nat.shape
    N = NT * P
    S = 4
    STEPS = 5
    GROUPS = B // S
    assert D == P and B % S == 0

    with ExitStack() as ctx:
        def sb(name, shape, dt=F32):
            return ctx.enter_context(nc.sbuf_tensor(name, [P, *shape], dt))

        def sem(name):
            return ctx.enter_context(nc.semaphore(name))

        x_all = sb("x_all", [B, NT, D])
        adjT = sb("adjT", [NT, N])
        adjT_hi = sb("adjT_hi", [NT, N], F32R)
        adjT_lo = sb("adjT_lo", [NT, N], F32R)
        adj2T_hi = sb("adj2T_hi", [NT, N], F32R)
        adj2T_lo = sb("adj2T_lo", [NT, N], F32R)
        mask = sb("mask", [NT, N])
        keep = sb("keep", [521])
        k = {n: keep[:, a:b] for n, (a, b) in KEEP.items()}
        ident = k["ident"]
        w3_hi, w3_lo = sb("w3_hi", [D], F32R), sb("w3_lo", [D], F32R)
        w43_hi, w43_lo = sb("w43_hi", [D], F32R), sb("w43_lo", [D], F32R)
        w5_hi, w5_lo = sb("w5_hi", [D], F32R), sb("w5_lo", [D], F32R)
        u5h = sb("u5h", [D])
        bias_z, bias_r, bias_h = sb("bias_z", [1]), sb("bias_r", [1]), sb("bias_h", [1])
        wx_hi, wx_lo = sb("wx_hi", [2 * D], F32R), sb("wx_lo", [2 * D], F32R)
        wu_hi, wu_lo = sb("wu_hi", [2 * D], F32R), sb("wu_lo", [2 * D], F32R)
        wa_src, wa_dst_rows = sb("wa_src", [1]), sb("wa_dst_rows", [D])
        a_i_rows, a_j_rows = sb("a_i_rows", [D]), sb("a_j_rows", [D])
        a_dst_rows = sb("a_dst_rows", [D])
        minus_half = sb("minus_half", [NT])
        carrier = sb("carrier", [10])
        w_sum = sb("w_sum", [3 * D])

        state = sb("state", [S, N])
        hT = [state[:, s, :] for s in range(S)]
        prob = state
        work = sb("work", [10, N])
        tz, tr, rh = work[:, 0:2, :], work[:, 2:4, :], work[:, 4:6, :]
        th, dh = work[:, 6:8, :], work[:, 8:10, :]
        probT = work[:, 0:4, :]
        e_hi, e_lo = work[:, 4:6, :], work[:, 6:8, :]
        temp = work[:, 0:4, :].rearrange("p a n -> p (a n)")
        w = {n: temp[:, a:b] for n, (a, b) in TEMP.items()}
        hN = sb("hN", [S, 2, NT, D], F32R)
        flat = hN[:, :, :, :, :].rearrange("p s a t d -> p s a (t d)")
        x2N_hi, x2N_lo = hN[:, 0, 0], hN[:, 0, 1]
        x2T_hi, x2T_lo = flat[:, 1, 0], flat[:, 1, 1]
        uT_hi, uT_lo = flat[:, 2, 0], flat[:, 2, 1]
        gN_hi, gN_lo = hN[:, 3, 0], hN[:, 3, 1]
        mT_hi, mT_lo = sb("mT_hi", [2, N], F32R), sb("mT_lo", [2, N], F32R)

        edge = sb("edge", [NT, N])
        x1N, x1T, gatN = sb("x1N", [NT, D]), sb("x1T", [N]), sb("gatN", [NT, D])
        attT, ex, rl, x2pre = sb("attT", [N]), sb("ex", [NT, D]), sb("rl", [NT, D]), sb("x2pre", [NT, D])
        x2N, y2T, x3pre = sb("x2N", [NT, D]), sb("y2T", [N]), sb("x3pre", [NT, D])
        x3N, x3T, scaled = sb("x3N", [NT, D]), sb("x3T", [N]), sb("scaled", [2, N])
        yN, sgT, x4pre = sb("yN", [NT, D]), sb("sgT", [N]), sb("x4pre", [NT, D])
        stats = [sb(f"stats{i}", [NT, 6]) for i in range(4)]
        moments = [sb(f"moments{i}", [NT, 2]) for i in range(4)]
        var_eps = [sb(f"var_eps{i}", [NT]) for i in range(4)]
        rstd = [sb(f"rstd{i}", [NT]) for i in range(4)]
        row_max, s_max, s_leak, shift = (sb(n, [NT]) for n in ("row_max", "s_max", "s_leak", "shift"))
        bias_1, bias_s, row_sum, row_inv = (sb(n, [NT]) for n in ("bias_1", "bias_s", "row_sum", "row_inv"))
        e_stats, e_mom = sb("e_stats", [2, 6]), sb("e_mom", [2, 2])
        e_mean, e_var, e_rstd = sb("e_mean", [1]), sb("e_var", [1]), sb("e_rstd", [1])
        c_norm, c_one = sb("c_norm", [NT]), sb("c_one", [NT])
        col_max, col_neg, col_shift = sb("col_max", [NT]), sb("col_neg", [NT]), sb("col_shift", [NT])
        col_sum, col_inv = sb("col_sum", [NT]), sb("col_inv", [NT])

        bank = [ctx.enter_context(nc.psum_tensor(f"bank{i}", [P, N], F32)) for i in range(8)]
        ps_m, ps_zr, ps_h, ps_t = bank[0:2], bank[2:4], bank[4:6], bank[6:8]
        A0, A1, A2, B0, B1, B2, C0, C1 = bank

        def tiles(b):
            return b[:, :].rearrange("p (t d) -> p t d", t=NT)

        s_keep, s_temp, s_adjT, s_adjN = sem("s_keep"), sem("s_temp"), sem("s_adjT"), sem("s_adjN")
        s_xN_first, s_xN_rest = sem("s_xN_first"), sem("s_xN_rest")
        s_xT = [sem(f"s_xT{s}") for s in range(S)]
        s_set, s_adst, s_wa, s_wad, s_wts_step, s_wts, s_adj_hi, s_adj_lo = (
            sem(n) for n in ("s_set", "s_adst", "s_wa", "s_wad", "s_wts_step", "s_wts", "s_adj_hi", "s_adj_lo"))
        s_adj2, s_adj2_hi, s_adj2_lo, s_mask = (sem(n) for n in ("s_adj2", "s_adj2_hi", "s_adj2_lo", "s_mask"))
        s_m, s_mhi, s_mlo, s_z, s_tz, s_r, s_tr, s_rh = (
            sem(n) for n in ("s_m", "s_mhi", "s_mlo", "s_z", "s_tz", "s_r", "s_tr", "s_rh"))
        s_h, s_th, s_dh, s_eh, s_new, s_t, s_nhi, s_nlo = (
            sem(n) for n in ("s_h", "s_th", "s_dh", "s_eh", "s_new", "s_t", "s_nhi", "s_nlo"))
        (s1_chain, s1_var, s1_rstd, s1_x, s1_T, s1_xT, s1_g, s1_gs, s1_d, s1_s, s1_b, s1_e, s1_p, s1_pT, s1_pA,
         s1_pD, s1_o, s1_oT, s1_oN, s1_inv, s1_ex, s1_var2, s1_rstd2, s1_x2) = (sem(f"s1_{n}") for n in (
            "chain", "var", "rstd", "x", "T", "xT", "g", "gs", "d", "s", "b", "e", "p", "pT", "pA",
            "pD", "o", "oT", "oN", "inv", "ex", "var2", "rstd2", "x2"))
        (s2_chain, s2_hi, s2_lo, s2_T, s2_Thi, s2_Tlo, s2_u, s2_uhi, s2_ulo, s2_g, s2_ghi, s2_glo, s2_y2, s2_yT,
         s2_yN, s2_y0, s2_pre, s2_var, s2_rstd, s2_x3) = (sem(f"s2_{n}") for n in (
            "chain", "hi", "lo", "T", "Thi", "Tlo", "u", "uhi", "ulo", "g", "ghi", "glo", "y2", "yT",
            "yN", "y0", "pre", "var", "rstd", "x3"))
        (s3_chain, s3_T, s3_xT, s3_p, s3_q, s3_qs, s3_qc, s3_var, s3_rstd, s3_c, s3_z, s3_e, s3_cm, s3_l, s3_E,
         s3_y, s3_o, s3_sg, s3_sg2, s3_oN, s3_free, s3_var4, s3_rstd4, s3_out) = (sem(f"s3_{n}") for n in (
            "chain", "T", "xT", "p", "q", "qs", "qc", "var", "rstd", "c", "z", "e", "cm", "l", "E",
            "y", "o", "sg", "sg2", "oN", "free", "var4", "rstd4", "out"))
        s_store = sem("s_store")

        def ticks(eng, layers):
            def tick(b, on):
                for slot in range(7):
                    for lag in (2, 1, 0):
                        if on[lag]:
                            layers[lag](slot, b - lag)
            tick(0, (True, False, False))
            tick(1, (True, True, False))
            with eng.Fori(2, B, 1) as b:
                tick(b, (True, True, True))
            tick(B, (False, True, True))
            tick(B + 1, (False, False, True))

        block = ctx.enter_context(nc.Block())

        @block.sync
        def _(sp):
            sp.dma_start(adjT[:, :, :], adj_tr).then_inc(s_adjT, 16)
            sp.dma_start(x_all[:, 0:S], x_nat[:, 0:S]).then_inc(s_xN_first, 16)
            sp.dma_start(keep[:, :], keep_pack).then_inc(s_keep, 16)
            sp.dma_start(temp[:, 0:temp_pack.shape[1]], temp_pack).then_inc(s_temp, 16)
            for s in range(S):
                sp.dma_start(hT[s], x_tr[:, s, :]).then_inc(s_xT[s], 16)
            sp.dma_start(edge[:, :, :], adj_nat).then_inc(s_adjN, 16)
            for g in range(1, GROUPS):
                sp.dma_start(x_all[:, g * S:(g + 1) * S], x_nat[:, g * S:(g + 1) * S]).then_inc(s_xN_rest, 16)
            with sp.Fori(1, GROUPS, 1) as g:
                for s in range(S):
                    sp.wait_ge(s_t, g * (STEPS * S) - S + s + 1)
                    sp.dma_start(hT[s], x_tr[:, bass.ds(g * S + s, 1), :].rearrange("p a n -> p (a n)")).then_inc(s_xT[s], 16)
            with sp.Fori(0, B, 1) as b:
                sp.wait_ge(s3_out, b + 1)
                sp.dma_start(out[:, bass.ds(b, 1)], x_all[:, bass.ds(b, 1)]).then_inc(s_store, 16)
            sp.wait_ge(s_store, 16 * B)

        @block.tensor
        def _(pe):
            mm = nc.tensor.matmul

            def split_mm(psum, wt_hi, wt_lo, mv_hi, mv_lo, start, stop):
                mm(psum, wt_hi, mv_hi, start=start, stop=False)
                mm(psum, wt_lo, mv_hi, start=False, stop=False)
                return mm(psum, wt_hi, mv_lo, start=False, stop=stop)

            def by_adj(psum, xN_hi, xN_lo, aT_hi, aT_lo):
                for j in range(NT):
                    mm(psum, xN_hi[:, j, :], aT_hi[:, j, :], start=(j == 0), stop=False)
                    mm(psum, xN_hi[:, j, :], aT_lo[:, j, :], start=False, stop=False)
                for j in range(NT):
                    last = mm(psum, xN_lo[:, j, :], aT_hi[:, j, :], start=False, stop=(j == NT - 1))
                return last

            def transposes(psum, src):
                for t in range(NT):
                    last = nc.tensor.transpose(psum[:, t * P:(t + 1) * P], src[:, t * P:(t + 1) * P], ident)
                return last

            pe.wait_ge(s_keep, 16)
            pe.wait_ge(s_temp, 16)
            pe.wait_ge(s_adst, 1)
            mm(bank[0][:, 0:1], w["w_gatT"], k["a_src"], start=True, stop=True)
            mm(bank[1][:, 0:D], w["w_gatT"], a_dst_rows[:, :], start=True, stop=True).then_inc(s_wa, 1)
            pe.wait_ge(s_wad, 1)
            pe.wait_ge(s_wts, 1)
            pe.wait_ge(s_adj_hi, 1)
            pe.wait_ge(s_adj_lo, 1)

            def messages(s, n):
                pe.wait_ge(s_nhi, n + s + 1)
                pe.wait_ge(s_nlo, n + s + 1)
                by_adj(ps_m[s % 2][:, :], hN[:, s, 0], hN[:, s, 1], adjT_hi, adjT_lo).then_inc(s_m, 1)

            def gates(s, n, loaded):
                i = s % 2
                zr = ps_zr[i][:, :]
                pe.wait_ge(s_xT[s], loaded)
                mm(zr, k["u3T"], hT[s], start=True, stop=False, skip_group_check=True)
                pe.wait_ge(s_mhi, n + s + 1)
                mm(zr, w3_hi[:, :], mT_hi[:, i], start=False, stop=False, skip_group_check=True)
                mm(zr, w3_lo[:, :], mT_hi[:, i], start=False, stop=False, skip_group_check=True)
                pe.wait_ge(s_mlo, n + s + 1)
                mm(zr, w3_hi[:, :], mT_lo[:, i], start=False, stop=True, skip_group_check=True).then_inc(s_z, 1)
                split_mm(ps_h[i][:, :], w5_hi[:, :], w5_lo[:, :], mT_hi[:, i], mT_lo[:, i], True, False)
                pe.wait_ge(s_tz, n + s + 1)
                mm(zr, w43_hi[:, :], mT_hi[:, i], start=False, stop=False, skip_group_check=True)
                mm(zr, w43_lo[:, :], mT_hi[:, i], start=False, stop=False, skip_group_check=True)
                mm(zr, w43_hi[:, :], mT_lo[:, i], start=False, stop=True, skip_group_check=True).then_inc(s_r, 1)

            def candidate(s, n):
                pe.wait_ge(s_rh, n + s + 1)
                mm(ps_h[s % 2][:, :], u5h[:, :], rh[:, s % 2], start=False, stop=True).then_inc(s_h, 1)

            def to_natural(s, n, act_read):
                pe.wait_ge(s_new, n + s + 1)
                pe.wait_ge(s_nlo, S + n + s - 1)
                if act_read:
                    pe.wait_ge(s_nhi, S + n + s - 1)
                transposes(ps_t[s % 2], hT[s]).then_inc(s_t, 1)

            def segment(n, loaded, loaded_next, final=False):
                for s in range(S):
                    more = not (final and s == S - 1)
                    after = (s + 1, n, loaded) if s + 1 < S else (0, n + S, loaded_next)
                    if more:
                        messages(after[0], after[1])
                    candidate(s, n)
                    if more:
                        gates(*after)
                    to_natural(s, n, act_read=not (final and s >= 2))

            messages(0, 0)
            gates(0, 0, 16)
            with pe.Fori(1, GROUPS, 1) as g:
                first = g * (STEPS * S) - STEPS * S
                with pe.Fori(first, first + (STEPS - 1) * S, S) as n:
                    segment(n, g * 16, g * 16)
                segment(first + (STEPS - 1) * S, g * 16, g * 16 + 16)
            with pe.Fori((GROUPS - 1) * STEPS * S, GROUPS * STEPS * S - S, S) as n:
                segment(n, GROUPS * 16, GROUPS * 16)
            segment(GROUPS * STEPS * S - S, GROUPS * 16, GROUPS * 16, final=True)

            pe.wait_ge(s_adjN, 16)
            pe.wait_ge(s_th, B * STEPS)
            pe.wait_ge(s_tr, B * STEPS)
            for j in range(NT):
                for q in range(NT):
                    last = mm(bank[j][:, :], edge[:, q, j * P:(j + 1) * P], adjT[:, q, :],
                              start=(q == 0), stop=(q == NT - 1))
                last.then_inc(s_adj2, 1)
            pe.wait_ge(s_nlo, B * STEPS + S)

            def attention(slot, b):
                if slot == 1:
                    if isinstance(b, int) and b == 0:
                        pe.wait_ge(s_adj2_lo, NT)
                        pe.wait_ge(s_adj2_hi, NT)
                    wait(pe, s1_x, b + 1)
                    transposes(A0, x1N[:, :, :].rearrange("p t d -> p (t d)")).then_inc(s1_T, 1)
                if slot == 2:
                    wait(pe, s1_xT, b + 1)
                    for t in range(NT):
                        last = mm(A1[:, t * D:(t + 1) * D], x1T[:, t * P:(t + 1) * P], k["w_gat"],
                                  start=True, stop=True)
                    last.then_inc(s1_g, 1)
                    mm(A2[:, :], wa_dst_rows[:, :], x1T[:, :], start=True, stop=True).then_inc(s1_d, 1)
                    for t in range(NT):
                        last = mm(A0[:, t:t + 1], x1T[:, t * P:(t + 1) * P], wa_src[:, :], start=True, stop=True)
                    last.then_inc(s1_s, 1)
                if slot == 4:
                    wait(pe, s1_p, b * NT + NT)

                    def turn(j):
                        if j >= 2:
                            wait(pe, s1_pA if j % 2 == 0 else s1_pD, b * 2 + j // 2)
                        psum = A0 if j % 2 == 0 else A2
                        for t in range(NT):
                            last = nc.tensor.transpose(psum[:, t * P:(t + 1) * P],
                                                       prob[:, t, j * P:(j + 1) * P], ident)
                        last.then_inc(s1_pT, 1)

                    turn(0)
                    turn(1)
                    wait(pe, s1_gs, b + 1)
                    for j in range(NT):
                        wait(pe, s1_pA if j % 2 == 0 else s1_pD, b * 2 + j // 2 + 1)
                        last = mm(A1[:, :], gatN[:, j, :], probT[:, j, :], start=(j == 0), stop=(j == NT - 1))
                        if j + 2 < NT:
                            turn(j + 2)
                    last.then_inc(s1_o, 1)
                if slot == 5:
                    wait(pe, s1_oT, b + 1)
                    transposes(A0, attT).then_inc(s1_oN, 1)

            def chebyshev(slot, b):
                if slot == 0:
                    wait(pe, s1_x2, b + 1)
                    wait(pe, s2_y0, b)
                    transposes(B0, x2N[:, :, :].rearrange("p t d -> p (t d)")).then_inc(s2_T, 1)
                if slot == 1:
                    wait(pe, s2_hi, b + 1)
                    wait(pe, s2_lo, b + 1)
                    wait(pe, s2_pre, b)
                    by_adj(B1[:, :], x2N_hi, x2N_lo, adjT_hi, adjT_lo).then_inc(s2_u, 1)
                if slot == 2:
                    wait(pe, s2_Thi, b + 1)
                    wait(pe, s2_Tlo, b + 1)
                    for t in range(NT):
                        psum = (B2, B0)[t // 2][:, (t % 2) * 2 * D:(t % 2 + 1) * 2 * D]
                        c = slice(t * P, (t + 1) * P)
                        split_mm(psum, x2T_hi[:, c], x2T_lo[:, c], wx_hi[:, :], wx_lo[:, :], True, False)
                        if t == 0:
                            wait(pe, s2_uhi, b + 1)
                            wait(pe, s2_ulo, b + 1)
                        last = split_mm(psum, uT_hi[:, c], uT_lo[:, c], wu_hi[:, :], wu_lo[:, :], False, True)
                        if t % 2:
                            last.then_inc(s2_g, 1)
                if slot == 4:
                    wait(pe, s2_ghi, b * 2 + 2)
                    wait(pe, s2_glo, b * 2 + 2)
                    by_adj(B1[:, :], gN_hi, gN_lo, adj2T_hi, adj2T_lo).then_inc(s2_y2, 1)
                if slot == 5:
                    wait(pe, s2_yT, b + 1)
                    transposes(B1, y2T).then_inc(s2_yN, 1)

            def edges(slot, b):
                if slot == 0:
                    wait(pe, s2_x3, b + 1)
                    transposes(C0, x3N[:, :, :].rearrange("p t d -> p (t d)")).then_inc(s3_T, 1)
                if slot == 1:
                    wait(pe, s3_xT, b + 1)
                    wait(pe, s3_free, b + 1)
                    mm(C1[:, :], a_i_rows[:, :], x3T[:, :], start=True, stop=True).then_inc(s3_p, 1)
                    mm(C0[:, :], a_j_rows[:, :], x3T[:, :], start=True, stop=True).then_inc(s3_q, 1)
                if slot == 2:
                    wait(pe, s3_qs, b + 1)
                    for t in range(NT):
                        last = mm(C0[:, t:t + 1], x3T[:, t * P:(t + 1) * P], k["a_j"], start=True, stop=True)
                    last.then_inc(s3_qc, 1)
                if slot == 4:
                    wait(pe, s3_y, b + 1)
                    for j in range(NT):
                        last = mm(C0[:, :], yN[:, j, :], edge[:, j, :], start=(j == 0), stop=(j == NT - 1))
                    last.then_inc(s3_o, 1)
                if slot == 5:
                    wait(pe, s3_sg2, b + 1)
                    transposes(C1, sgT).then_inc(s3_oN, 1)

            ticks(pe, (attention, chebyshev, edges))

        @block.scalar
        def _(act):
            def copy(dst, src):
                return nc.scalar.activation(dst, src, ACT.Copy)

            act.wait_ge(s_adjT, 16)
            copy(adjT_hi[:, :, :], adjT[:, :, :]).then_inc(s_adj_hi, 1)
            act.wait_ge(s_xN_first, 16)
            for s in range(S):
                copy(hN[:, s, 0], x_all[:, s]).then_inc(s_nhi, 1)
            act.wait_ge(s_set, 1)

            def messages(s, n):
                act.wait_ge(s_m, n + s + 1)
                copy(mT_hi[:, s % 2], ps_m[s % 2][:, :]).then_inc(s_mhi, 1)

            def gates(s, n):
                i = s % 2
                act.wait_ge(s_z, n + s + 1)
                nc.scalar.activation(tz[:, i], ps_zr[i][:, :], ACT.Tanh, bias=bias_z[:, :], scale=0.5).then_inc(s_tz, 1)
                act.wait_ge(s_r, n + s + 1)
                nc.scalar.activation(tr[:, i], ps_zr[i][:, :], ACT.Tanh, bias=bias_r[:, :], scale=0.5).then_inc(s_tr, 1)

            def candidate(s, n):
                act.wait_ge(s_h, n + s + 1)
                nc.scalar.activation(th[:, s % 2], ps_h[s % 2][:, :], ACT.Tanh, bias=bias_h[:, :]).then_inc(s_th, 1)

            def segment(n, next_x=None, final=False):
                for s in range(S):
                    more = not (final and s == S - 1)
                    after = (s + 1, n) if s + 1 < S else (0, n + S)
                    if more:
                        messages(*after)
                    candidate(s, n)
                    if more:
                        gates(*after)
                    if final:
                        continue
                    act.wait_ge(s_t, n + s + 1)
                    src = tiles(ps_t[s % 2]) if next_x is None else \
                        x_all[:, bass.ds(next_x + s, 1)].rearrange("p a t d -> p (a t) d")
                    copy(hN[:, s, 0], src).then_inc(s_nhi, 1)

            messages(0, 0)
            gates(0, 0)
            act.wait_ge(s_xN_rest, 16 * (GROUPS - 1))
            with act.Fori(1, GROUPS, 1) as g:
                first = g * (STEPS * S) - STEPS * S
                with act.Fori(first, first + (STEPS - 1) * S, S) as n:
                    segment(n)
                segment(first + (STEPS - 1) * S, next_x=g * S)
            with act.Fori((GROUPS - 1) * STEPS * S, GROUPS * STEPS * S - S, S) as n:
                segment(n)
            segment(GROUPS * STEPS * S - S, final=True)

            for j in range(NT):
                act.wait_ge(s_adj2, j + 1)
                copy(adj2T_hi[:, j, :], bank[j][:, :]).then_inc(s_adj2_hi, 1)

            def attention(slot, b):
                if slot == 1:
                    wait(act, s1_T, b + 1)
                    copy(x1T[:, :], A0[:, :]).then_inc(s1_xT, 1)
                if slot == 2:
                    wait(act, s1_g, b + 1)
                    copy(gatN[:, :, :], tiles(A1)).then_inc(s1_gs, 1)
                if slot == 3:
                    wait(act, s1_b, b + 1)
                    for t in range(NT):
                        if t >= 2:
                            wait(act, s1_p, b * NT + t - 1)
                        nc.scalar.activation(e_hi[:, t % 2], state[:, t, :], ACT.Exp, bias=bias_1[:, t:t + 1])
                        nc.scalar.activation(e_lo[:, t % 2], state[:, t, :], ACT.Exp, bias=bias_s[:, t:t + 1],
                                             scale=SLOPE).then_inc(s1_e, 1)
                if slot == 4:
                    for j in (0, 2):
                        wait(act, s1_pT, b * NT + j + 1)
                        copy(probT[:, j, :], A0[:, :]).then_inc(s1_pA, 1)
                if slot == 5:
                    wait(act, s1_o, b + 1)
                    copy(attT[:, :], A1[:, :]).then_inc(s1_oT, 1)
                if slot == 6:
                    wait(act, s1_inv, b + 1)
                    wait(act, s1_oN, b + 1)
                    for t in range(NT):
                        last = nc.scalar.activation(ex[:, t, :], A0[:, t * D:(t + 1) * D], ACT.Exp,
                                                    scale=row_inv[:, t:t + 1])
                    last.then_inc(s1_ex, 1)

            def chebyshev(slot, b):
                if slot == 0:
                    wait(act, s1_x2, b + 1)
                    copy(x2N_hi, x2N[:, :, :]).then_inc(s2_hi, 1)
                    wait(act, s2_T, b + 1)
                    copy(x2T_hi, B0[:, :]).then_inc(s2_Thi, 1)
                if slot == 1:
                    wait(act, s2_u, b + 1)
                    copy(uT_hi, B1[:, :]).then_inc(s2_uhi, 1)
                if slot == 2:
                    for q, psum in enumerate((B2, B0)):
                        wait(act, s2_g, b * 2 + q + 1)
                        copy(gN_hi[:, 2 * q:2 * q + 2, :],
                             psum[:, :].rearrange("p (t k d) -> p t k d", t=2, k=2)[:, :, 0, :]).then_inc(s2_ghi, 1)
                if slot == 4:
                    wait(act, s2_y2, b + 1)
                    copy(y2T[:, :], B1[:, :]).then_inc(s2_yT, 1)

            def edges(slot, b):
                if slot == 0:
                    wait(act, s3_T, b + 1)
                    copy(x3T[:, :], C0[:, :]).then_inc(s3_xT, 1)
                if slot == 3:
                    wait(act, s3_c, b + 1)
                    for j in range(NT):
                        if j >= 2:
                            wait(act, s3_e, b * NT + j - 1)
                        nc.scalar.activation(scaled[:, j % 2], C1[:, :], ACT.Identity, bias=c_one[:, j:j + 1],
                                             scale=e_rstd[:, :]).then_inc(s3_z, 1)
                    wait(act, s3_cm, b + 1)
                    for j in range(NT):
                        wait(act, s3_l, b * NT + j + 1)
                        nc.scalar.activation(edge[:, j, :], edge[:, j, :], ACT.Exp, bias=col_shift[:, j:j + 1],
                                             accum_out=col_sum[:, j:j + 1]).then_inc(s3_E, 1)
                if slot == 5:
                    wait(act, s3_o, b + 1)
                    nc.scalar.activation(sgT[:, :], C0[:, :], ACT.Tanh, scale=0.5).then_inc(s3_sg, 1)

            ticks(act, (attention, chebyshev, edges))

        @block.vector
        def _(dve):
            tt, ts = nc.vector.tensor_tensor, nc.vector.tensor_scalar
            stt, cp = nc.vector.scalar_tensor_tensor, nc.vector.tensor_copy
            low = nc.vector.tensor_tensor

            def rest(dst, whole, hi):
                return low(dst, whole, hi.bitcast(F32), ALU.subtract)

            def carry(site):
                nc.vector.memset(carrier[:, site:site + 1], 0.0)

            nc.vector.memset(minus_half[:, :], -0.5).then_inc(s3_free, 1)
            dve.wait_ge(s_keep, 16)
            dve.wait_ge(s_temp, 16)

            def rows(dst, col):
                return ts(dst, ident, 0.0, col, ALU.mult, ALU.add)

            rows(a_dst_rows[:, :], k["a_dst"]).then_inc(s_adst, 1)
            rows(a_i_rows[:, :], k["a_i"])
            rows(a_j_rows[:, :], k["a_j"])
            tt(w_sum[:, 0:D], w["w3T"][:, 0:D], w["w3T"][:, D:2 * D], ALU.add)
            tt(w_sum[:, D:2 * D], w["w4T"][:, 0:D], w["w4T"][:, D:2 * D], ALU.add)
            tt(w_sum[:, 2 * D:3 * D], w["w5T"][:, 0:D], w["w5T"][:, D:2 * D], ALU.add)
            tt(bias_z[:, :], k["w3_b"], k["u3_b"], ALU.add)
            tt(bias_r[:, :], k["w4_b"], k["u3_b"], ALU.add)
            tt(bias_h[:, :], k["w5_b"], k["u5_b"], ALU.add).then_inc(s_wts_step, 1)
            dve.wait_ge(s_wts_step, 1)
            ts(u5h[:, :], k["u5T"], 0.5, None, ALU.mult)
            ts(bias_z[:, :], bias_z[:, :], 0.5, None, ALU.mult)
            ts(bias_r[:, :], bias_r[:, :], 0.5, None, ALU.mult).then_inc(s_set, 1)
            cp(w3_hi[:, :], w_sum[:, 0:D])
            cp(w5_hi[:, :], w_sum[:, 2 * D:3 * D])
            tt(w_sum[:, D:2 * D], w_sum[:, D:2 * D], w_sum[:, 0:D], ALU.subtract).then_inc(s_wts_step, 1)
            dve.wait_ge(s_wts_step, 2)
            cp(w43_hi[:, :], w_sum[:, D:2 * D])
            rest(w3_lo[:, :], w_sum[:, 0:D], w3_hi[:, :])
            rest(w5_lo[:, :], w_sum[:, 2 * D:3 * D], w5_hi[:, :]).then_inc(s_wts_step, 1)
            dve.wait_ge(s_wts_step, 3)
            rest(w43_lo[:, :], w_sum[:, D:2 * D], w43_hi[:, :]).then_inc(s_wts_step, 1)
            cheb = w["cheb"].rearrange("p (k d) -> p k d", d=D)
            for i in (1, 2, 3):
                last = tt(cheb[:, i], cheb[:, i], cheb[:, i + 3], ALU.add)
            last.then_inc(s_wts_step, 1)
            dve.wait_ge(s_wts_step, 5)
            for hi, (g_at, y_at) in ((wx_hi, (2, 0)), (wu_hi, (3, 1))):
                cp(hi[:, 0:D], cheb[:, g_at])
                last = cp(hi[:, D:2 * D], cheb[:, y_at])
            last.then_inc(s_wts_step, 1)
            dve.wait_ge(s_wts_step, 6)
            for lo, hi, (g_at, y_at) in ((wx_lo, wx_hi, (2, 0)), (wu_lo, wu_hi, (3, 1))):
                rest(lo[:, 0:D], cheb[:, g_at], hi[:, 0:D])
                last = rest(lo[:, D:2 * D], cheb[:, y_at], hi[:, D:2 * D])
            last.then_inc(s_wts, 1)
            dve.wait_ge(s_adj_hi, 1)
            rest(adjT_lo[:, :, :], adjT[:, :, :], adjT_hi[:, :, :]).then_inc(s_adj_lo, 1)
            dve.wait_ge(s_wa, 1)
            cp(wa_src[:, :], bank[0][:, 0:1])
            cp(wa_dst_rows[:, :], bank[1][:, 0:D]).then_inc(s_wad, 1)
            for s in range(S):
                dve.wait_ge(s_nhi, s + 1)
                rest(hN[:, s, 1], x_all[:, s], hN[:, s, 0]).then_inc(s_nlo, 1)

            def messages(s, n):
                dve.wait_ge(s_mhi, n + s + 1)
                rest(mT_lo[:, s % 2], ps_m[s % 2][:, :], mT_hi[:, s % 2]).then_inc(s_mlo, 1)

            def reset(s, n):
                dve.wait_ge(s_tr, n + s + 1)
                stt(rh[:, s % 2], tr[:, s % 2], 1.0, hT[s], ALU.add, ALU.mult).then_inc(s_rh, 1)

            def update(s, n):
                i = s % 2
                dve.wait_ge(s_th, n + s + 1)
                tt(dh[:, i], th[:, i], hT[s], ALU.subtract).then_inc(s_dh, 1)
                dve.wait_ge(s_dh, n + s + 1)
                stt(dh[:, i], tz[:, i], 1.0, dh[:, i], ALU.add, ALU.mult).then_inc(s_eh, 1)
                dve.wait_ge(s_eh, n + s + 1)
                stt(hT[s], dh[:, i], 0.5, hT[s], ALU.mult, ALU.add).then_inc(s_new, 1)

            def segment(n, this_x=None, final=False):
                for s in range(S):
                    more = not (final and s == S - 1)
                    after = (s + 1, n) if s + 1 < S else (0, n + S)
                    if more:
                        messages(*after)
                    update(s, n)
                    if more:
                        reset(*after)
                    dve.wait_ge(s_t, n + s + 1)
                    if this_x is None:
                        dve.wait_ge(s_nhi, S + n + s + 1)
                        rest(hN[:, s, 1], tiles(ps_t[s % 2]), hN[:, s, 0]).then_inc(s_nlo, 1)
                        continue
                    x = x_all[:, bass.ds(this_x + s, 1)].rearrange("p a t d -> p (a t) d")
                    last = tt(x, x, tiles(ps_t[s % 2]), ALU.add)
                    if not final:
                        x = x_all[:, bass.ds(this_x + s + S, 1)].rearrange("p a t d -> p (a t) d")
                        dve.wait_ge(s_nhi, S + n + s + 1)
                        last = rest(hN[:, s, 1], x, hN[:, s, 0])
                    last.then_inc(s_nlo, 1)

            messages(0, 0)
            reset(0, 0)
            dve.wait_ge(s_xN_rest, 16 * (GROUPS - 1))
            with dve.Fori(1, GROUPS, 1) as g:
                first = g * (STEPS * S) - STEPS * S
                with dve.Fori(first, first + (STEPS - 1) * S, S) as n:
                    segment(n)
                segment(first + (STEPS - 1) * S, this_x=g * S - S)
            with dve.Fori((GROUPS - 1) * STEPS * S, GROUPS * STEPS * S - S, S) as n:
                segment(n)
            segment(GROUPS * STEPS * S - S, this_x=B - S, final=True)

            dve.wait_ge(s_adjN, 16)
            cp(mask[:, :, :], edge[:, :, :]).then_inc(s_mask, 1)
            dve.wait_ge(s_mask, 1)
            for t in range(NT):
                last = tt(mask[:, t, t * P:(t + 1) * P], mask[:, t, t * P:(t + 1) * P], ident, ALU.add)
            last.then_inc(s_mask, 1)
            dve.wait_ge(s_mask, 2)
            ts(mask[:, :, :], mask[:, :, :], 0.0, MASKED, ALU.is_le, ALU.mult).then_inc(s_mask, 1)
            for j in range(NT):
                dve.wait_ge(s_adj2_hi, j + 1)
                rest(adj2T_lo[:, j, :], bank[j][:, :], adj2T_hi[:, j, :]).then_inc(s_adj2_lo, 1)

            def layer_norm(i, b, chain, src, dst, s_var, s_rstd, s_done, stage=0):
                for t in range(NT):
                    last = nc.vector.bn_stats(stats[i][:, t, :], src(t))
                chain.link(last)
                carry(i)
                for t in range(NT):
                    last = nc.vector.bn_aggr(moments[i][:, t, :], stats[i][:, t, :])
                chain.link(last)
                ts(var_eps[i][:, :], moments[i][:, :, 1], LN_EPS, None, ALU.add).then_inc(s_var, 1)
                wait(dve, s_rstd, b + 1)
                for t in range(NT):
                    last = ts(dst(t), src(t), moments[i][:, t, 0:1], rstd[i][:, t:t + 1], ALU.subtract, ALU.mult)
                last.then_inc(s_done, 1)

            def graph(b):
                x = x_all[:, bass.ds(b, 1)].rearrange("p a t d -> p (a t) d")
                return lambda t: x[:, t, :]

            def tile_of(x):
                return lambda t: x[:, t, :]

            chains = {}

            def attention(slot, b):
                if slot == 0:
                    chains[1] = c = Chain(dve, s1_chain, 11, b)
                    layer_norm(0, b, c, graph(b), tile_of(x1N), s1_var, s1_rstd, s1_x)
                c = chains.get(1)
                if slot == 2:
                    wait(dve, s1_d, b + 1)
                    carry(5)
                    for t in range(NT):
                        last = nc.vector.tensor_tensor_reduce(state[:, t, :], A2[:, :], mask[:, t, :], 1.0, MASKED,
                                                              ALU.add, ALU.max, row_max[:, t:t + 1])
                    c.link(last)
                    wait(dve, s1_s, b + 1)
                    c.link(tt(s_max[:, :], A0[:, 0:NT], row_max[:, :], ALU.add))
                    c.link(ts(s_leak[:, :], s_max[:, :], SLOPE, None, ALU.mult))
                    c.link(tt(shift[:, :], s_max[:, :], s_leak[:, :], ALU.max))
                    tt(bias_1[:, :], A0[:, 0:NT], shift[:, :], ALU.subtract)
                    stt(bias_s[:, :], A0[:, 0:NT], SLOPE, shift[:, :], ALU.mult, ALU.subtract).then_inc(s1_b, 1)
                if slot == 3:
                    for t in range(NT):
                        wait(dve, s1_e, b * NT + t + 1)
                        stt(prob[:, t, :], e_hi[:, t % 2], 1.0, e_lo[:, t % 2], ALU.mult, ALU.max,
                            accum_out=row_sum[:, t:t + 1]).then_inc(s1_p, 1)
                if slot == 4:
                    wait(dve, s1_p, b * NT + NT)
                    nc.vector.reciprocal(row_inv[:, :], row_sum[:, :]).then_inc(s1_inv, 1)
                    for j in (1, 3):
                        wait(dve, s1_pT, b * NT + j + 1)
                        cp(probT[:, j, :], A2[:, :]).then_inc(s1_pD, 1)
                if slot == 6:
                    wait(dve, s1_ex, b + 1)
                    for t in range(NT):
                        last = ts(rl[:, t, :], A0[:, t * D:(t + 1) * D], row_inv[:, t:t + 1], 0.0, ALU.mult, ALU.max)
                    c.link(last)
                    c.link(stt(rl[:, :, :], ex[:, :, :], 1.0, rl[:, :, :], ALU.min, ALU.add))
                    c.link(stt(x2pre[:, :, :], rl[:, :, :], -1.0, x1N[:, :, :], ALU.add, ALU.add))
                    layer_norm(1, b, c, tile_of(x2pre), tile_of(x2N), s1_var2, s1_rstd2, s1_x2)
                    c.close()

            def chebyshev(slot, b):
                if slot == 0:
                    chains[2] = Chain(dve, s2_chain, 2, b)
                    wait(dve, s2_hi, b + 1)
                    rest(x2N_lo, x2N[:, :, :], x2N_hi).then_inc(s2_lo, 1)
                    wait(dve, s2_Thi, b + 1)
                    rest(x2T_lo, B0[:, :], x2T_hi).then_inc(s2_Tlo, 1)
                if slot == 1:
                    wait(dve, s2_uhi, b + 1)
                    rest(uT_lo, B1[:, :], uT_hi).then_inc(s2_ulo, 1)
                if slot in (2, 4):
                    for q, psum in enumerate((B2, B0)):
                        sums = psum[:, :].rearrange("p (t k d) -> p t k d", t=2, k=2)
                        two = slice(2 * q, 2 * q + 2)
                        if slot == 2:
                            wait(dve, s2_ghi, b * 2 + q + 1)
                            rest(gN_lo[:, two, :], sums[:, :, 0, :], gN_hi[:, two, :]).then_inc(s2_glo, 1)
                        else:
                            last = tt(x3pre[:, two, :], sums[:, :, 1, :], x2N[:, two, :], ALU.add)
                    if slot == 4:
                        last.then_inc(s2_y0, 1)
                if slot == 6:
                    wait(dve, s2_yN, b + 1)
                    wait(dve, s2_y0, b + 1)
                    tt(x3pre[:, :, :], tiles(B1), x3pre[:, :, :], ALU.add).then_inc(s2_pre, 1)
                    wait(dve, s2_pre, b + 1)
                    layer_norm(2, b, chains[2], tile_of(x3pre), tile_of(x3N), s2_var, s2_rstd, s2_x3)
                    chains[2].close()

            def edges(slot, b):
                if slot == 0:
                    chains[3] = Chain(dve, s3_chain, 6, b)
                c = chains.get(3)
                if slot == 2:
                    wait(dve, s3_p, b + 1)
                    nc.vector.bn_stats(e_stats[:, 0, :], C1[:, :])
                    wait(dve, s3_q, b + 1)
                    nc.vector.bn_stats(e_stats[:, 1, :], C0[:, :]).then_inc(s3_qs, 1)
                    wait(dve, s3_qs, b + 1)
                    carry(4)
                    nc.vector.bn_aggr(e_mom[:, 0, :], e_stats[:, 0, :])
                    c.link(nc.vector.bn_aggr(e_mom[:, 1, :], e_stats[:, 1, :]))
                    tt(e_mean[:, :], e_mom[:, 0, 0:1], e_mom[:, 1, 0:1], ALU.add)
                    stt(e_var[:, :], e_mom[:, 0, 1:2], EDGE_EPS, e_mom[:, 1, 1:2], ALU.add, ALU.add).then_inc(s3_var, 1)
                    wait(dve, s3_rstd, b + 1)
                    wait(dve, s3_qc, b + 1)
                    c.link(ts(c_norm[:, :], C0[:, 0:NT], e_mean[:, :], e_rstd[:, :], ALU.subtract, ALU.mult))
                    ts(c_one[:, :], c_norm[:, :], 1.0, None, ALU.add).then_inc(s3_c, 1)
                if slot == 3:
                    for j in range(NT):
                        wait(dve, s3_z, b * NT + j + 1)
                        carry(6 + j)
                        nc.vector.tensor_tensor_reduce(edge[:, j, :], scaled[:, j % 2], adjT[:, j, :], 1.0, -3.0e38,
                                                       ALU.mult, ALU.max, col_max[:, j:j + 1]).then_inc(s3_e, 1)
                    wait(dve, s3_e, b * NT + NT)
                    c.link(ts(col_neg[:, :], col_max[:, :], -1.0, None, ALU.mult))
                    stt(col_shift[:, :], col_max[:, :], -SLOPE, col_neg[:, :], ALU.mult, ALU.min).then_inc(s3_cm, 1)
                    for j in range(NT):
                        stt(edge[:, j, :], edge[:, j, :], SLOPE, edge[:, j, :], ALU.mult, ALU.max).then_inc(s3_l, 1)
                if slot == 4:
                    wait(dve, s3_E, b * NT + NT)
                    c.link(nc.vector.reciprocal(col_inv[:, :], col_sum[:, :]))
                    for j in range(NT):
                        last = ts(yN[:, j, :], x3N[:, j, :], col_inv[:, j:j + 1], None, ALU.mult)
                    last.then_inc(s3_y, 1)
                if slot == 5:
                    wait(dve, s3_sg, b + 1)
                    ts(sgT[:, :], sgT[:, :], 0.5, 0.5, ALU.mult, ALU.add).then_inc(s3_sg2, 1)
                if slot == 6:
                    wait(dve, s3_oN, b + 1)
                    tt(x4pre[:, :, :], tiles(C1), x3N[:, :, :], ALU.add).then_inc(s3_free, 1)
                    wait(dve, s3_free, b + 2)
                    layer_norm(3, b, c, tile_of(x4pre), graph(b), s3_var4, s3_rstd4, s3_out)
                    c.close()

            ticks(dve, (attention, chebyshev, edges))

        @block.gpsimd
        def _(pool):
            pool.wait_ge(s3_free, 1)

            def root(s_var, s_rstd, src, dst, b):
                wait(pool, s_var, b + 1)
                nc.gpsimd.tensor_tensor(dst, src, minus_half[:, 0:dst.shape[1]], ALU.pow).then_inc(s_rstd, 1)

            def attention(slot, b):
                if slot == 0:
                    root(s1_var, s1_rstd, var_eps[0][:, :], rstd[0][:, :], b)
                if slot == 6:
                    root(s1_var2, s1_rstd2, var_eps[1][:, :], rstd[1][:, :], b)

            def chebyshev(slot, b):
                if slot == 6:
                    root(s2_var, s2_rstd, var_eps[2][:, :], rstd[2][:, :], b)

            def edges(slot, b):
                if slot == 2:
                    root(s3_var, s3_rstd, e_var[:, :], e_rstd[:, :], b)
                if slot == 6:
                    root(s3_var4, s3_rstd4, var_eps[3][:, :], rstd[3][:, :], b)

            ticks(pool, (attention, chebyshev, edges))


def kernel(x, adj, L0_gnn_w3_w, L0_gnn_w3_b, L0_gnn_u3_w, L0_gnn_u3_b, L0_gnn_w4_w, L0_gnn_w4_b, L0_gnn_w5_w,
           L0_gnn_w5_b, L0_gnn_u5_w, L0_gnn_u5_b, L1_gnn_W, L1_gnn_a_src, L1_gnn_a_dst, L2_gnn_weight_1, L3_gnn_a):
    import numpy as np
    import concourse.bacc as bacc
    from concourse.bass_utils import run_bass_kernel_spmd

    x = np.asarray(x)
    B, N, D = x.shape
    NT = N // P

    def nodes_first(a):
        return np.asarray(a).reshape(NT, P, -1).transpose(1, 0, 2)

    def halves(a):
        return np.asarray(a).reshape(D, 2, D).transpose(2, 1, 0).reshape(D, 2 * D)

    def col(a):
        return np.asarray(a).reshape(D, -1)

    a = np.asarray(L3_gnn_a)
    keep = dict(u3T=np.asarray(L0_gnn_u3_w).T, w_gat=np.asarray(L1_gnn_W), ident=np.eye(P, dtype=np.float32),
                a_src=col(L1_gnn_a_src), a_dst=col(L1_gnn_a_dst), a_i=a[:D], a_j=a[D:], w3_b=col(L0_gnn_w3_b),
                u3_b=col(L0_gnn_u3_b), w4_b=col(L0_gnn_w4_b), w5_b=col(L0_gnn_w5_b), u5_b=col(L0_gnn_u5_b),
                u5T=np.asarray(L0_gnn_u5_w).T)
    temp = dict(w3T=halves(L0_gnn_w3_w), w4T=halves(L0_gnn_w4_w), w5T=halves(L0_gnn_w5_w),
                cheb=np.asarray(L2_gnn_weight_1).transpose(0, 2, 1).reshape(D, -1), w_gatT=np.asarray(L1_gnn_W).T)
    arrays = dict(
        x_nat=x.reshape(B, NT, P, D).transpose(2, 0, 1, 3),
        x_tr=x.transpose(2, 0, 1),
        adj_nat=nodes_first(adj),
        adj_tr=nodes_first(np.asarray(adj).T),
        keep_pack=np.concatenate([keep[n] for n in KEEP], axis=1),
        temp_pack=np.concatenate([temp[n] for n in TEMP], axis=1),
    )
    arrays = {n: np.ascontiguousarray(v) for n, v in arrays.items()}
    nc = bacc.Bacc("TRN2", target_bir_lowering=False, num_devices=1)
    aps = {n: nc.dram_tensor(n, v.shape, F32, kind="ExternalInput").ap() for n, v in arrays.items()}
    aps["out"] = nc.dram_tensor("out", (P, B, NT, D), F32, kind="ExternalOutput").ap()
    build(nc, **aps)
    got = run_bass_kernel_spmd(nc, [arrays], core_ids=[0]).results[0]["out"]
    return np.ascontiguousarray(np.asarray(got).reshape(P, B, NT, D).transpose(1, 2, 0, 3).reshape(B, N, D))
```

```python
from contextlib import ExitStack

import concourse.bass as bass
from concourse import mybir

F32 = mybir.dt.float32
F32R = mybir.dt.float32r
ALU = mybir.AluOpType
ACT = mybir.ActivationFunctionType

P = 128
LN_EPS = 1e-5
EDGE_EPS = 1e-14
SLOPE = 0.2
MASKED = -(2.0**100)

KEEP = dict(u3T=(0, 128), w_gat=(128, 256), ident=(256, 384), a_src=(384, 385), a_dst=(385, 386),
            a_i=(386, 387), a_j=(387, 388), w3_b=(388, 389), u3_b=(389, 390), w4_b=(390, 391),
            w5_b=(391, 392), u5_b=(392, 393), u5T=(393, 521))
TEMP = dict(w3T=(0, 256), w4T=(256, 512), w5T=(512, 768), cheb=(768, 1664), w_gatT=(1664, 1792))


def wait(eng, sem, value):
    if not (isinstance(value, int) and value <= 0):
        eng.wait_ge(sem, value)


class Chain:

    def __init__(self, eng, sem, per, at):
        self.eng, self.sem, self.per, self.at, self.n = eng, sem, per, at, 0

    def link(self, instruction):
        self.n += 1
        instruction.then_inc(self.sem, 1)
        self.eng.wait_ge(self.sem, self.at * self.per + self.n)

    def close(self):
        assert self.n == self.per


def build(nc, x_nat, x_tr, adj_nat, adj_tr, keep_pack, temp_pack, out):
    _, B, NT, D = x_nat.shape
    N = NT * P
    S = 4
    STEPS = 5
    GROUPS = B // S
    assert D == P and B % S == 0

    with ExitStack() as ctx:
        def sb(name, shape, dt=F32):
            return ctx.enter_context(nc.sbuf_tensor(name, [P, *shape], dt))

        def sem(name):
            return ctx.enter_context(nc.semaphore(name))

        x_all = sb("x_all", [B, NT, D])
        adjT = sb("adjT", [NT, N])
        adjT_hi = sb("adjT_hi", [NT, N], F32R)
        adjT_lo = sb("adjT_lo", [NT, N], F32R)
        adj2T = sb("adj2T", [NT, N])
        mask = sb("mask", [NT, N])
        keep = sb("keep", [521])
        k = {n: keep[:, a:b] for n, (a, b) in KEEP.items()}
        ident = k["ident"]
        w3_hi, w3_lo = sb("w3_hi", [D], F32R), sb("w3_lo", [D], F32R)
        w43_hi, w43_lo = sb("w43_hi", [D], F32R), sb("w43_lo", [D], F32R)
        w5_hi, w5_lo = sb("w5_hi", [D], F32R), sb("w5_lo", [D], F32R)
        u5h = sb("u5h", [D])
        bias_z, bias_r, bias_h = sb("bias_z", [1]), sb("bias_r", [1]), sb("bias_h", [1])
        w_cheb = sb("w_cheb", [4 * D])
        w_x, w_u = w_cheb[:, 0:2 * D], w_cheb[:, 2 * D:4 * D]
        wa_src, wa_dst_rows = sb("wa_src", [1]), sb("wa_dst_rows", [D])
        a_i_rows, a_j_rows = sb("a_i_rows", [D]), sb("a_j_rows", [D])
        a_dst_rows = sb("a_dst_rows", [D])
        minus_half = sb("minus_half", [NT])
        carrier = sb("carrier", [10])
        w_sum = sb("w_sum", [3 * D])

        state = sb("state", [S, N])
        hT = [state[:, s, :] for s in range(S)]
        prob = state
        work = sb("work", [10, N])
        tz, tr, rh = work[:, 0:2, :], work[:, 2:4, :], work[:, 4:6, :]
        th, dh = work[:, 6:8, :], work[:, 8:10, :]
        probT = work[:, 0:4, :]
        e_hi, e_lo = work[:, 4:6, :], work[:, 6:8, :]
        temp = work[:, 0:4, :].rearrange("p a n -> p (a n)")
        w = {n: temp[:, a:b] for n, (a, b) in TEMP.items()}
        hN = sb("hN", [S, 2, NT, D], F32R)
        x2N_hi, x2N_lo = hN[:, 0, 0], hN[:, 0, 1]
        mT_hi, mT_lo = sb("mT_hi", [2, N], F32R), sb("mT_lo", [2, N], F32R)

        edge = sb("edge", [NT, N])
        x1N, x1T, gatN = sb("x1N", [NT, D]), sb("x1T", [N]), sb("gatN", [NT, D])
        attT, ex, rl, x2pre = sb("attT", [N]), sb("ex", [NT, D]), sb("rl", [NT, D]), sb("x2pre", [NT, D])
        x2T, uT, gN = sb("x2T", [N]), sb("uT", [N]), sb("gN", [NT, D])
        x2N, y2T, x3pre = sb("x2N", [NT, D]), sb("y2T", [N]), sb("x3pre", [NT, D])
        x3N, x3T, scaled = sb("x3N", [NT, D]), sb("x3T", [N]), sb("scaled", [2, N])
        yN, sgT, x4pre = sb("yN", [NT, D]), sb("sgT", [N]), sb("x4pre", [NT, D])
        stats = [sb(f"stats{i}", [NT, 6]) for i in range(4)]
        moments = [sb(f"moments{i}", [NT, 2]) for i in range(4)]
        var_eps = [sb(f"var_eps{i}", [NT]) for i in range(4)]
        rstd = [sb(f"rstd{i}", [NT]) for i in range(4)]
        row_max, s_max, s_leak, shift = (sb(n, [NT]) for n in ("row_max", "s_max", "s_leak", "shift"))
        bias_1, bias_s, row_sum, row_inv = (sb(n, [NT]) for n in ("bias_1", "bias_s", "row_sum", "row_inv"))
        e_stats, e_mom = sb("e_stats", [2, 6]), sb("e_mom", [2, 2])
        e_mean, e_var, e_rstd = sb("e_mean", [1]), sb("e_var", [1]), sb("e_rstd", [1])
        c_norm, c_one = sb("c_norm", [NT]), sb("c_one", [NT])
        col_max, col_neg, col_shift = sb("col_max", [NT]), sb("col_neg", [NT]), sb("col_shift", [NT])
        col_sum, col_inv = sb("col_sum", [NT]), sb("col_inv", [NT])

        bank = [ctx.enter_context(nc.psum_tensor(f"bank{i}", [P, N], F32)) for i in range(8)]
        ps_m, ps_zr, ps_h, ps_t = bank[0:2], bank[2:4], bank[4:6], bank[6:8]
        A0, A1, A2, B0, B1, B2, C0, C1 = bank

        def tiles(b):
            return b[:, :].rearrange("p (t d) -> p t d", t=NT)

        s_keep, s_temp, s_adjT, s_adjN = sem("s_keep"), sem("s_temp"), sem("s_adjT"), sem("s_adjN")
        s_xN_first, s_xN_rest = sem("s_xN_first"), sem("s_xN_rest")
        s_xT = [sem(f"s_xT{s}") for s in range(S)]
        s_set, s_adst, s_wa, s_wad, s_wts_step, s_wts, s_adj_hi, s_adj_lo = (
            sem(n) for n in ("s_set", "s_adst", "s_wa", "s_wad", "s_wts_step", "s_wts", "s_adj_hi", "s_adj_lo"))
        s_adj2, s_adj2c, s_mask = (sem(n) for n in ("s_adj2", "s_adj2c", "s_mask"))
        s_m, s_mhi, s_mlo, s_z, s_tz, s_r, s_tr, s_rh = (
            sem(n) for n in ("s_m", "s_mhi", "s_mlo", "s_z", "s_tz", "s_r", "s_tr", "s_rh"))
        s_h, s_th, s_dh, s_eh, s_new, s_t, s_nhi, s_nlo = (
            sem(n) for n in ("s_h", "s_th", "s_dh", "s_eh", "s_new", "s_t", "s_nhi", "s_nlo"))
        def sems(prefix, names):
            return [sem(f"{prefix}_{n}") for n in names.split()]

        s_ln, s_ln_chain, s_ln_var, s_ln_rstd = (
            [sem(f"{n}{i}") for i in range(4)] for n in ("s_ln", "s_ln_chain", "s_ln_var", "s_ln_rstd"))
        (s1_chain, s1_T, s1_xT, s1_g, s1_gs, s1_d, s1_s, s1_t, s1_b, s1_e, s1_p, s1_pT, s1_pc, s1_o, s1_oT, s1_oN,
         s1_inv, s1_ex, s1_rl, s1_elu, s1_pre) = sems(
            "s1", "chain T xT g gs d s t b e p pT pc o oT oN inv ex rl elu pre")
        s2_hi, s2_lo, s2_T, s2_xT, s2_u, s2_uT, s2_g, s2_gN, s2_y2, s2_yT, s2_yN, s2_y0, s2_pre = sems(
            "s2", "hi lo T xT u uT g gN y2 yT yN y0 pre")
        (s3_chain, s3_cchain, s3_mchain, s3_T, s3_xT, s3_p, s3_q, s3_qs, s3_qc, s3_var, s3_rstd, s3_c, s3_z, s3_e,
         s3_cm, s3_l, s3_E, s3_inv, s3_y, s3_o, s3_sg, s3_sg2, s3_oN, s3_free) = sems(
            "s3", "chain cchain mchain T xT p q qs qc var rstd c z e cm l E inv y o sg sg2 oN free")
        s_store = sem("s_store")

        LAG = 4

        def ticks(eng, order):
            def tick(t):
                for stage, lag, *args in order:
                    b = t - lag
                    if not isinstance(b, int) or 0 <= b < B:
                        stage(b, *args)
            for t in range(LAG + 1):
                tick(t)
            with eng.Fori(LAG + 1, B, 1) as t:
                tick(t)
            for t in range(B, B + LAG):
                tick(t)

        block = ctx.enter_context(nc.Block())

        @block.sync
        def _(sp):
            sp.dma_start(adjT[:, :, :], adj_tr).then_inc(s_adjT, 16)
            sp.dma_start(x_all[:, 0:S], x_nat[:, 0:S]).then_inc(s_xN_first, 16)
            sp.dma_start(keep[:, :], keep_pack).then_inc(s_keep, 16)
            sp.dma_start(temp[:, 0:temp_pack.shape[1]], temp_pack).then_inc(s_temp, 16)
            for s in range(S):
                sp.dma_start(hT[s], x_tr[:, s, :]).then_inc(s_xT[s], 16)
            sp.dma_start(edge[:, :, :], adj_nat).then_inc(s_adjN, 16)
            for g in range(1, GROUPS):
                sp.dma_start(x_all[:, g * S:(g + 1) * S], x_nat[:, g * S:(g + 1) * S]).then_inc(s_xN_rest, 16)
            with sp.Fori(1, GROUPS, 1) as g:
                for s in range(S):
                    sp.wait_ge(s_t, g * (STEPS * S) - S + s + 1)
                    sp.dma_start(hT[s], x_tr[:, bass.ds(g * S + s, 1), :].rearrange("p a n -> p (a n)")).then_inc(s_xT[s], 16)
            with sp.Fori(0, B, 1) as b:
                sp.wait_ge(s_ln[3], b + 1)
                sp.dma_start(out[:, bass.ds(b, 1)], x_all[:, bass.ds(b, 1)]).then_inc(s_store, 16)
            sp.wait_ge(s_store, 16 * B)

        @block.tensor
        def _(pe):
            mm = nc.tensor.matmul

            def split_mm(psum, wt_hi, wt_lo, mv_hi, mv_lo, start, stop):
                mm(psum, wt_hi, mv_hi, start=start, stop=False)
                mm(psum, wt_lo, mv_hi, start=False, stop=False)
                return mm(psum, wt_hi, mv_lo, start=False, stop=stop)

            def by_adj(psum, xN_hi, xN_lo, aT_hi, aT_lo):
                for j in range(NT):
                    mm(psum, xN_hi[:, j, :], aT_hi[:, j, :], start=(j == 0), stop=False)
                    mm(psum, xN_hi[:, j, :], aT_lo[:, j, :], start=False, stop=False)
                for j in range(NT):
                    last = mm(psum, xN_lo[:, j, :], aT_hi[:, j, :], start=False, stop=(j == NT - 1))
                return last

            def transposes(psum, src):
                for t in range(NT):
                    last = nc.tensor.transpose(psum[:, t * P:(t + 1) * P], src[:, t * P:(t + 1) * P], ident)
                return last

            pe.wait_ge(s_keep, 16)
            pe.wait_ge(s_temp, 16)
            pe.wait_ge(s_adst, 1)
            mm(bank[0][:, 0:1], w["w_gatT"], k["a_src"], start=True, stop=True)
            mm(bank[1][:, 0:D], w["w_gatT"], a_dst_rows[:, :], start=True, stop=True).then_inc(s_wa, 1)
            pe.wait_ge(s_wad, 1)
            pe.wait_ge(s_wts, 1)
            pe.wait_ge(s_adj_hi, 1)
            pe.wait_ge(s_adj_lo, 1)

            def messages(s, n):
                pe.wait_ge(s_nhi, n + s + 1)
                pe.wait_ge(s_nlo, n + s + 1)
                by_adj(ps_m[s % 2][:, :], hN[:, s, 0], hN[:, s, 1], adjT_hi, adjT_lo).then_inc(s_m, 1)

            def gates(s, n, loaded):
                i = s % 2
                zr = ps_zr[i][:, :]
                pe.wait_ge(s_xT[s], loaded)
                mm(zr, k["u3T"], hT[s], start=True, stop=False, skip_group_check=True)
                pe.wait_ge(s_mhi, n + s + 1)
                mm(zr, w3_hi[:, :], mT_hi[:, i], start=False, stop=False, skip_group_check=True)
                mm(zr, w3_lo[:, :], mT_hi[:, i], start=False, stop=False, skip_group_check=True)
                pe.wait_ge(s_mlo, n + s + 1)
                mm(zr, w3_hi[:, :], mT_lo[:, i], start=False, stop=True, skip_group_check=True).then_inc(s_z, 1)
                split_mm(ps_h[i][:, :], w5_hi[:, :], w5_lo[:, :], mT_hi[:, i], mT_lo[:, i], True, False)
                pe.wait_ge(s_tz, n + s + 1)
                mm(zr, w43_hi[:, :], mT_hi[:, i], start=False, stop=False, skip_group_check=True)
                mm(zr, w43_lo[:, :], mT_hi[:, i], start=False, stop=False, skip_group_check=True)
                mm(zr, w43_hi[:, :], mT_lo[:, i], start=False, stop=True, skip_group_check=True).then_inc(s_r, 1)

            def candidate(s, n):
                pe.wait_ge(s_rh, n + s + 1)
                mm(ps_h[s % 2][:, :], u5h[:, :], rh[:, s % 2], start=False, stop=True).then_inc(s_h, 1)

            def to_natural(s, n, act_read):
                pe.wait_ge(s_new, n + s + 1)
                pe.wait_ge(s_nlo, S + n + s - 1)
                if act_read:
                    pe.wait_ge(s_nhi, S + n + s - 1)
                transposes(ps_t[s % 2], hT[s]).then_inc(s_t, 1)

            def segment(n, loaded, loaded_next, final=False):
                for s in range(S):
                    more = not (final and s == S - 1)
                    after = (s + 1, n, loaded) if s + 1 < S else (0, n + S, loaded_next)
                    if more:
                        messages(after[0], after[1])
                    candidate(s, n)
                    if more:
                        gates(*after)
                    to_natural(s, n, act_read=not (final and s >= 2))

            messages(0, 0)
            gates(0, 0, 16)
            with pe.Fori(1, GROUPS, 1) as g:
                first = g * (STEPS * S) - STEPS * S
                with pe.Fori(first, first + (STEPS - 1) * S, S) as n:
                    segment(n, g * 16, g * 16)
                segment(first + (STEPS - 1) * S, g * 16, g * 16 + 16)
            with pe.Fori((GROUPS - 1) * STEPS * S, GROUPS * STEPS * S - S, S) as n:
                segment(n, GROUPS * 16, GROUPS * 16)
            segment(GROUPS * STEPS * S - S, GROUPS * 16, GROUPS * 16, final=True)

            pe.wait_ge(s_adjN, 16)
            pe.wait_ge(s_th, B * STEPS)
            pe.wait_ge(s_tr, B * STEPS)
            for j in range(NT):
                for q in range(NT):
                    last = mm(bank[j][:, :], edge[:, q, j * P:(j + 1) * P], adjT[:, q, :],
                              start=(q == 0), stop=(q == NT - 1))
                last.then_inc(s_adj2, 1)
            pe.wait_ge(s_adj2c, NT)
            pe.wait_ge(s_nlo, B * STEPS + S)

            def flat_(x):
                return x[:, :, :].rearrange("p t d -> p (t d)")

            def x1_turn(b):
                wait(pe, s_ln[0], b + 1)
                transposes(A0, flat_(x1N)).then_inc(s1_T, 1)

            def near_row(b):
                wait(pe, s1_xT, b + 1)
                mm(A2[:, :], wa_dst_rows[:, :], x1T[:, :], start=True, stop=True).then_inc(s1_d, 1)

            def own_col(b):
                wait(pe, s1_xT, b + 1)
                for t in range(NT):
                    last = mm(A0[:, t:t + 1], x1T[:, t * P:(t + 1) * P], wa_src[:, :], start=True, stop=True)
                last.then_inc(s1_s, 1)

            def project(b):
                wait(pe, s1_xT, b + 1)
                for t in range(NT):
                    last = mm(A1[:, t * D:(t + 1) * D], x1T[:, t * P:(t + 1) * P], k["w_gat"], start=True, stop=True)
                last.then_inc(s1_g, 1)

            def prob_turn(j):
                for t in range(NT):
                    last = nc.tensor.transpose((A0, A2)[j % 2][:, t * P:(t + 1) * P],
                                               prob[:, t, j * P:(j + 1) * P], ident)
                last.then_inc(s1_pT, 1)

            def prob_turns(b):
                wait(pe, s1_p, b * NT + NT)
                prob_turn(0)
                prob_turn(1)

            def attend(b, j):
                if j == 0:
                    wait(pe, s1_gs, b + 1)
                wait(pe, s1_pc, b * NT + j + 1)
                if j + 2 < NT:
                    prob_turn(j + 2)
                last = mm(A1[:, :], gatN[:, j, :], probT[:, j, :], start=(j == 0), stop=(j == NT - 1))
                if j == NT - 1:
                    last.then_inc(s1_o, 1)

            def att_turn(b):
                wait(pe, s1_oT, b + 1)
                transposes(A0, attT).then_inc(s1_oN, 1)

            def x2_turn(b):
                wait(pe, s_ln[1], b + 1)
                transposes(B0, flat_(x2N)).then_inc(s2_T, 1)

            def once(b):
                wait(pe, s2_hi, b + 1)
                wait(pe, s2_lo, b + 1)
                wait(pe, s2_pre, b)
                by_adj(B1[:, :], x2N_hi, x2N_lo, adjT_hi, adjT_lo).then_inc(s2_u, 1)

            def weigh(b):
                wait(pe, s2_xT, b + 1)
                wait(pe, s2_uT, b + 1)
                for t in range(NT):
                    psum = (B2, B0)[t // 2][:, (t % 2) * 2 * D:(t % 2 + 1) * 2 * D]
                    mm(psum, x2T[:, t * P:(t + 1) * P], w_x, start=True, stop=False)
                    last = mm(psum, uT[:, t * P:(t + 1) * P], w_u, start=False, stop=True)
                last.then_inc(s2_g, 1)

            def twice(b):
                wait(pe, s2_gN, b + 1)
                for j in range(NT):
                    last = mm(B1[:, :], gN[:, j, :], adj2T[:, j, :], start=(j == 0), stop=(j == NT - 1))
                last.then_inc(s2_y2, 1)

            def y2_turn(b):
                wait(pe, s2_yT, b + 1)
                transposes(B1, y2T).then_inc(s2_yN, 1)

            def x3_turn(b):
                wait(pe, s_ln[2], b + 1)
                transposes(C0, flat_(x3N)).then_inc(s3_T, 1)

            def pair_rows(b):
                wait(pe, s3_xT, b + 1)
                wait(pe, s3_free, b + 1)
                mm(C1[:, :], a_i_rows[:, :], x3T[:, :], start=True, stop=True).then_inc(s3_p, 1)
                mm(C0[:, :], a_j_rows[:, :], x3T[:, :], start=True, stop=True).then_inc(s3_q, 1)

            def q_col(b):
                wait(pe, s3_qs, b + 1)
                for t in range(NT):
                    last = mm(C0[:, t:t + 1], x3T[:, t * P:(t + 1) * P], k["a_j"], start=True, stop=True)
                last.then_inc(s3_qc, 1)

            def gather(b):
                wait(pe, s3_y, b + 1)
                for j in range(NT):
                    last = mm(C0[:, :], yN[:, j, :], edge[:, j, :], start=(j == 0), stop=(j == NT - 1))
                last.then_inc(s3_o, 1)

            def sig_turn(b):
                wait(pe, s3_sg2, b + 1)
                transposes(C1, sgT).then_inc(s3_oN, 1)

            ticks(pe, ((sig_turn, 4), (project, 1), (once, 2), (x3_turn, 3), (prob_turns, 1), (pair_rows, 3),
                 (attend, 1, 0), (attend, 1, 1), (q_col, 3), (attend, 1, 2), (attend, 1, 3),
                 (att_turn, 1), (weigh, 2), (twice, 2), (x1_turn, 0), (near_row, 0), (own_col, 0),
                 (y2_turn, 2), (gather, 3), (x2_turn, 1)))

        @block.scalar
        def _(act):
            def copy(dst, src):
                return nc.scalar.activation(dst, src, ACT.Copy)

            act.wait_ge(s_adjT, 16)
            copy(adjT_hi[:, :, :], adjT[:, :, :]).then_inc(s_adj_hi, 1)
            act.wait_ge(s_xN_first, 16)
            for s in range(S):
                copy(hN[:, s, 0], x_all[:, s]).then_inc(s_nhi, 1)
            act.wait_ge(s_set, 1)

            def messages(s, n):
                act.wait_ge(s_m, n + s + 1)
                copy(mT_hi[:, s % 2], ps_m[s % 2][:, :]).then_inc(s_mhi, 1)

            def gates(s, n):
                i = s % 2
                act.wait_ge(s_z, n + s + 1)
                nc.scalar.activation(tz[:, i], ps_zr[i][:, :], ACT.Tanh, bias=bias_z[:, :], scale=0.5).then_inc(s_tz, 1)
                act.wait_ge(s_r, n + s + 1)
                nc.scalar.activation(tr[:, i], ps_zr[i][:, :], ACT.Tanh, bias=bias_r[:, :], scale=0.5).then_inc(s_tr, 1)

            def candidate(s, n):
                act.wait_ge(s_h, n + s + 1)
                nc.scalar.activation(th[:, s % 2], ps_h[s % 2][:, :], ACT.Tanh, bias=bias_h[:, :]).then_inc(s_th, 1)

            def segment(n, next_x=None, final=False):
                for s in range(S):
                    more = not (final and s == S - 1)
                    after = (s + 1, n) if s + 1 < S else (0, n + S)
                    if more:
                        messages(*after)
                    candidate(s, n)
                    if more:
                        gates(*after)
                    if final:
                        continue
                    act.wait_ge(s_t, n + s + 1)
                    src = tiles(ps_t[s % 2]) if next_x is None else \
                        x_all[:, bass.ds(next_x + s, 1)].rearrange("p a t d -> p (a t) d")
                    copy(hN[:, s, 0], src).then_inc(s_nhi, 1)

            messages(0, 0)
            gates(0, 0)
            act.wait_ge(s_xN_rest, 16 * (GROUPS - 1))
            with act.Fori(1, GROUPS, 1) as g:
                first = g * (STEPS * S) - STEPS * S
                with act.Fori(first, first + (STEPS - 1) * S, S) as n:
                    segment(n)
                segment(first + (STEPS - 1) * S, next_x=g * S)
            with act.Fori((GROUPS - 1) * STEPS * S, GROUPS * STEPS * S - S, S) as n:
                segment(n)
            segment(GROUPS * STEPS * S - S, final=True)

            for j in range(NT):
                act.wait_ge(s_adj2, j + 1)
                copy(adj2T[:, j, :], bank[j][:, :]).then_inc(s_adj2c, 1)

            def x1_cols(b):
                wait(act, s1_T, b + 1)
                copy(x1T[:, :], A0[:, :]).then_inc(s1_xT, 1)

            def projected(b):
                wait(act, s1_g, b + 1)
                copy(gatN[:, :, :], tiles(A1)).then_inc(s1_gs, 1)

            def line_exps(b, t):
                if t == 0:
                    wait(act, s1_b, b + 1)
                if t >= 2:
                    wait(act, s1_p, b * NT + t - 1)
                nc.scalar.activation(e_hi[:, t % 2], state[:, t, :], ACT.Exp, bias=bias_1[:, t:t + 1])
                nc.scalar.activation(e_lo[:, t % 2], state[:, t, :], ACT.Exp, bias=bias_s[:, t:t + 1],
                                     scale=SLOPE).then_inc(s1_e, 1)

            def prob_cols(b, j):
                wait(act, s1_pT, b * NT + j + 1)
                copy(probT[:, j, :], (A0, A2)[j % 2][:, :]).then_inc(s1_pc, 1)

            def attended(b):
                wait(act, s1_o, b + 1)
                copy(attT[:, :], A1[:, :]).then_inc(s1_oT, 1)

            def elu_parts(b, func, dst, done):
                wait(act, s1_inv, b + 1)
                wait(act, s1_oN, b + 1)
                for t in range(NT):
                    last = nc.scalar.activation(dst[:, t, :], A0[:, t * D:(t + 1) * D], func,
                                                scale=row_inv[:, t:t + 1])
                last.then_inc(done, 1)

            def elu_exp(b):
                elu_parts(b, ACT.Exp, ex, s1_ex)

            def elu_relu(b):
                elu_parts(b, ACT.Relu, rl, s1_rl)

            def x2_high(b):
                wait(act, s_ln[1], b + 1)
                copy(x2N_hi, x2N[:, :, :]).then_inc(s2_hi, 1)

            def x2_cols(b):
                wait(act, s2_T, b + 1)
                copy(x2T[:, :], B0[:, :]).then_inc(s2_xT, 1)

            def u_cols(b):
                wait(act, s2_u, b + 1)
                copy(uT[:, :], B1[:, :]).then_inc(s2_uT, 1)

            def g_rows(b):
                wait(act, s2_g, b + 1)
                for q, psum in enumerate((B2, B0)):
                    last = copy(gN[:, 2 * q:2 * q + 2, :],
                                psum[:, :].rearrange("p (t k d) -> p t k d", t=2, k=2)[:, :, 0, :])
                last.then_inc(s2_gN, 1)

            def y2_cols(b):
                wait(act, s2_y2, b + 1)
                copy(y2T[:, :], B1[:, :]).then_inc(s2_yT, 1)

            def x3_cols(b):
                wait(act, s3_T, b + 1)
                copy(x3T[:, :], C0[:, :]).then_inc(s3_xT, 1)

            def normed(b, j):
                if j == 0:
                    wait(act, s3_c, b + 1)
                if j >= 2:
                    wait(act, s3_e, b * NT + j - 1)
                nc.scalar.activation(scaled[:, j % 2], C1[:, :], ACT.Identity, bias=c_one[:, j:j + 1],
                                     scale=e_rstd[:, :]).then_inc(s3_z, 1)

            def edge_exp(b, j):
                if j == 0:
                    wait(act, s3_cm, b + 1)
                wait(act, s3_l, b * NT + j + 1)
                nc.scalar.activation(edge[:, j, :], edge[:, j, :], ACT.Exp, bias=col_shift[:, j:j + 1],
                                     accum_out=col_sum[:, j:j + 1]).then_inc(s3_E, 1)

            def shares(b):
                wait(act, s3_inv, b + 1)
                for j in range(NT):
                    last = nc.scalar.activation(yN[:, j, :], x3N[:, j, :], ACT.Copy, scale=col_inv[:, j:j + 1])
                last.then_inc(s3_y, 1)

            def sigmoid(b):
                wait(act, s3_o, b + 1)
                nc.scalar.activation(sgT[:, :], C0[:, :], ACT.Tanh, scale=0.5).then_inc(s3_sg, 1)
                wait(act, s3_sg, b + 1)
                nc.scalar.activation(sgT[:, :], sgT[:, :], ACT.Copy, scale=0.5, bias=0.5).then_inc(s3_sg2, 1)

            ticks(act, ((line_exps, 1, 0), (sigmoid, 4), (line_exps, 1, 1), (line_exps, 1, 2),
                  (line_exps, 1, 3), (projected, 1), (x3_cols, 3), (prob_cols, 1, 0), (prob_cols, 1, 1),
                  (prob_cols, 1, 2), (u_cols, 2), (x2_cols, 2), (prob_cols, 1, 3), (normed, 3, 0),
                  (normed, 3, 1), (attended, 1), (normed, 3, 2), (normed, 3, 3), (elu_relu, 1),
                  (elu_exp, 1), (g_rows, 2), (edge_exp, 3, 0), (edge_exp, 3, 1), (edge_exp, 3, 2),
                  (edge_exp, 3, 3), (x1_cols, 0), (y2_cols, 2), (shares, 3), (x2_high, 1)))

        @block.vector
        def _(dve):
            tt, ts = nc.vector.tensor_tensor, nc.vector.tensor_scalar
            stt, cp = nc.vector.scalar_tensor_tensor, nc.vector.tensor_copy
            low = nc.vector.tensor_tensor

            def rest(dst, whole, hi):
                return low(dst, whole, hi.bitcast(F32), ALU.subtract)

            def carry(site):
                nc.vector.memset(carrier[:, site:site + 1], 0.0)

            nc.vector.memset(minus_half[:, :], -0.5).then_inc(s3_free, 1)
            dve.wait_ge(s_keep, 16)
            dve.wait_ge(s_temp, 16)

            def rows(dst, col):
                return ts(dst, ident, 0.0, col, ALU.mult, ALU.add)

            rows(a_dst_rows[:, :], k["a_dst"]).then_inc(s_adst, 1)
            rows(a_i_rows[:, :], k["a_i"])
            rows(a_j_rows[:, :], k["a_j"])
            tt(w_sum[:, 0:D], w["w3T"][:, 0:D], w["w3T"][:, D:2 * D], ALU.add)
            tt(w_sum[:, D:2 * D], w["w4T"][:, 0:D], w["w4T"][:, D:2 * D], ALU.add)
            tt(w_sum[:, 2 * D:3 * D], w["w5T"][:, 0:D], w["w5T"][:, D:2 * D], ALU.add)
            tt(bias_z[:, :], k["w3_b"], k["u3_b"], ALU.add)
            tt(bias_r[:, :], k["w4_b"], k["u3_b"], ALU.add)
            tt(bias_h[:, :], k["w5_b"], k["u5_b"], ALU.add).then_inc(s_wts_step, 1)
            dve.wait_ge(s_wts_step, 1)
            ts(u5h[:, :], k["u5T"], 0.5, None, ALU.mult)
            ts(bias_z[:, :], bias_z[:, :], 0.5, None, ALU.mult)
            ts(bias_r[:, :], bias_r[:, :], 0.5, None, ALU.mult).then_inc(s_set, 1)
            cp(w3_hi[:, :], w_sum[:, 0:D])
            cp(w5_hi[:, :], w_sum[:, 2 * D:3 * D])
            tt(w_sum[:, D:2 * D], w_sum[:, D:2 * D], w_sum[:, 0:D], ALU.subtract).then_inc(s_wts_step, 1)
            dve.wait_ge(s_wts_step, 2)
            cp(w43_hi[:, :], w_sum[:, D:2 * D])
            rest(w3_lo[:, :], w_sum[:, 0:D], w3_hi[:, :])
            rest(w5_lo[:, :], w_sum[:, 2 * D:3 * D], w5_hi[:, :]).then_inc(s_wts_step, 1)
            dve.wait_ge(s_wts_step, 3)
            rest(w43_lo[:, :], w_sum[:, D:2 * D], w43_hi[:, :]).then_inc(s_wts_step, 1)
            cheb = w["cheb"].rearrange("p (k d) -> p k d", d=D)
            cp(w_cheb[:, D:2 * D], cheb[:, 0])
            for power, at in ((2, 0), (3, 2), (1, 3)):
                last = tt(w_cheb[:, at * D:(at + 1) * D], cheb[:, power], cheb[:, power + 3], ALU.add)
            last.then_inc(s_wts, 1)
            dve.wait_ge(s_adj_hi, 1)
            rest(adjT_lo[:, :, :], adjT[:, :, :], adjT_hi[:, :, :]).then_inc(s_adj_lo, 1)
            dve.wait_ge(s_wa, 1)
            cp(wa_src[:, :], bank[0][:, 0:1])
            cp(wa_dst_rows[:, :], bank[1][:, 0:D]).then_inc(s_wad, 1)
            for s in range(S):
                dve.wait_ge(s_nhi, s + 1)
                rest(hN[:, s, 1], x_all[:, s], hN[:, s, 0]).then_inc(s_nlo, 1)

            def messages(s, n):
                dve.wait_ge(s_mhi, n + s + 1)
                rest(mT_lo[:, s % 2], ps_m[s % 2][:, :], mT_hi[:, s % 2]).then_inc(s_mlo, 1)

            def reset(s, n):
                dve.wait_ge(s_tr, n + s + 1)
                stt(rh[:, s % 2], tr[:, s % 2], 1.0, hT[s], ALU.add, ALU.mult).then_inc(s_rh, 1)

            def update(s, n):
                i = s % 2
                dve.wait_ge(s_th, n + s + 1)
                tt(dh[:, i], th[:, i], hT[s], ALU.subtract).then_inc(s_dh, 1)
                dve.wait_ge(s_dh, n + s + 1)
                stt(dh[:, i], tz[:, i], 1.0, dh[:, i], ALU.add, ALU.mult).then_inc(s_eh, 1)
                dve.wait_ge(s_eh, n + s + 1)
                stt(hT[s], dh[:, i], 0.5, hT[s], ALU.mult, ALU.add).then_inc(s_new, 1)

            def segment(n, this_x=None, final=False):
                for s in range(S):
                    more = not (final and s == S - 1)
                    after = (s + 1, n) if s + 1 < S else (0, n + S)
                    if more:
                        messages(*after)
                    update(s, n)
                    if more:
                        reset(*after)
                    dve.wait_ge(s_t, n + s + 1)
                    if this_x is None:
                        dve.wait_ge(s_nhi, S + n + s + 1)
                        rest(hN[:, s, 1], tiles(ps_t[s % 2]), hN[:, s, 0]).then_inc(s_nlo, 1)
                        continue
                    x = x_all[:, bass.ds(this_x + s, 1)].rearrange("p a t d -> p (a t) d")
                    last = tt(x, x, tiles(ps_t[s % 2]), ALU.add)
                    if not final:
                        x = x_all[:, bass.ds(this_x + s + S, 1)].rearrange("p a t d -> p (a t) d")
                        dve.wait_ge(s_nhi, S + n + s + 1)
                        last = rest(hN[:, s, 1], x, hN[:, s, 0])
                    last.then_inc(s_nlo, 1)

            messages(0, 0)
            reset(0, 0)
            dve.wait_ge(s_xN_rest, 16 * (GROUPS - 1))
            with dve.Fori(1, GROUPS, 1) as g:
                first = g * (STEPS * S) - STEPS * S
                with dve.Fori(first, first + (STEPS - 1) * S, S) as n:
                    segment(n)
                segment(first + (STEPS - 1) * S, this_x=g * S - S)
            with dve.Fori((GROUPS - 1) * STEPS * S, GROUPS * STEPS * S - S, S) as n:
                segment(n)
            segment(GROUPS * STEPS * S - S, this_x=B - S, final=True)

            dve.wait_ge(s_adjN, 16)
            cp(mask[:, :, :], edge[:, :, :]).then_inc(s_mask, 1)
            dve.wait_ge(s_mask, 1)
            for t in range(NT):
                last = tt(mask[:, t, t * P:(t + 1) * P], mask[:, t, t * P:(t + 1) * P], ident, ALU.add)
            last.then_inc(s_mask, 1)
            dve.wait_ge(s_mask, 2)
            ts(mask[:, :, :], mask[:, :, :], 0.0, MASKED, ALU.is_le, ALU.mult).then_inc(s_mask, 1)
            dve.wait_ge(s_mask, 3)
            def graph(b):
                x = x_all[:, bass.ds(b, 1)].rearrange("p a t d -> p (a t) d")
                return lambda t: x[:, t, :]

            def tile_of(x):
                return lambda t: x[:, t, :]

            def ln_source(b, i):
                return (graph(b), tile_of(x2pre), tile_of(x3pre), tile_of(x4pre))[i]

            def moments_of(b, i):
                if i == 1:
                    wait(dve, s1_pre, b + 1)
                if i == 2:
                    wait(dve, s2_pre, b + 1)
                if i == 3:
                    wait(dve, s3_free, b + 2)
                wait(dve, s_ln[i], b)
                src = ln_source(b, i)
                chain = Chain(dve, s_ln_chain[i], 2, b)
                for t in range(NT):
                    last = nc.vector.bn_stats(stats[i][:, t, :], src(t))
                chain.link(last)
                carry(i)
                for t in range(NT):
                    last = nc.vector.bn_aggr(moments[i][:, t, :], stats[i][:, t, :])
                chain.link(last)
                chain.close()
                ts(var_eps[i][:, :], moments[i][:, :, 1], LN_EPS, None, ALU.add).then_inc(s_ln_var[i], 1)

            def normalise(b, i):
                src, dst = ln_source(b, i), (tile_of(x1N), tile_of(x2N), tile_of(x3N), graph(b))[i]
                wait(dve, s_ln_rstd[i], b + 1)
                if i == 0:
                    wait(dve, s1_pre, b)
                if i == 1:
                    wait(dve, s2_y0, b)
                if i == 2:
                    wait(dve, s3_free, b + 1)
                for t in range(NT):
                    last = ts(dst(t), src(t), moments[i][:, t, 0:1], rstd[i][:, t:t + 1], ALU.subtract, ALU.mult)
                last.then_inc(s_ln[i], 1)

            def scores(b):
                wait(dve, s1_d, b + 1)
                carry(5)
                for t in range(NT):
                    last = nc.vector.tensor_tensor_reduce(state[:, t, :], A2[:, :], mask[:, t, :], 1.0, MASKED,
                                                          ALU.add, ALU.max, row_max[:, t:t + 1])
                last.then_inc(s1_t, 1)

            def shifts(b):
                c = Chain(dve, s1_chain, 3, b)
                wait(dve, s1_t, b + 1)
                wait(dve, s1_s, b + 1)
                c.link(tt(s_max[:, :], A0[:, 0:NT], row_max[:, :], ALU.add))
                c.link(ts(s_leak[:, :], s_max[:, :], SLOPE, None, ALU.mult))
                c.link(tt(shift[:, :], s_max[:, :], s_leak[:, :], ALU.max))
                c.close()
                tt(bias_1[:, :], A0[:, 0:NT], shift[:, :], ALU.subtract)
                stt(bias_s[:, :], A0[:, 0:NT], SLOPE, shift[:, :], ALU.mult, ALU.subtract).then_inc(s1_b, 1)

            def probabilities(b, t):
                wait(dve, s1_e, b * NT + t + 1)
                stt(prob[:, t, :], e_hi[:, t % 2], 1.0, e_lo[:, t % 2], ALU.mult, ALU.max,
                    accum_out=row_sum[:, t:t + 1]).then_inc(s1_p, 1)

            def row_inverse(b):
                wait(dve, s1_p, b * NT + NT)
                nc.vector.reciprocal(row_inv[:, :], row_sum[:, :]).then_inc(s1_inv, 1)

            def elu_residual(b):
                wait(dve, s1_ex, b + 1)
                wait(dve, s1_rl, b + 1)
                wait(dve, s_ln[1], b)
                stt(rl[:, :, :], ex[:, :, :], 1.0, rl[:, :, :], ALU.min, ALU.add).then_inc(s1_elu, 1)
                wait(dve, s1_elu, b + 1)
                stt(x2pre[:, :, :], rl[:, :, :], -1.0, x1N[:, :, :], ALU.add, ALU.add).then_inc(s1_pre, 1)

            def y0_residual(b):
                wait(dve, s2_gN, b + 1)
                wait(dve, s_ln[2], b)
                for q, psum in enumerate((B2, B0)):
                    two = slice(2 * q, 2 * q + 2)
                    last = tt(x3pre[:, two, :], psum[:, :].rearrange("p (t k d) -> p t k d", t=2, k=2)[:, :, 1, :],
                              x2N[:, two, :], ALU.add)
                last.then_inc(s2_y0, 1)

            def y2_residual(b):
                wait(dve, s2_y0, b + 1)
                wait(dve, s2_yN, b + 1)
                tt(x3pre[:, :, :], tiles(B1), x3pre[:, :, :], ALU.add).then_inc(s2_pre, 1)

            def pair_moments(b):
                c = Chain(dve, s3_chain, 1, b)
                wait(dve, s3_p, b + 1)
                nc.vector.bn_stats(e_stats[:, 0, :], C1[:, :])
                wait(dve, s3_q, b + 1)
                nc.vector.bn_stats(e_stats[:, 1, :], C0[:, :]).then_inc(s3_qs, 1)
                wait(dve, s3_qs, b + 1)
                carry(4)
                nc.vector.bn_aggr(e_mom[:, 0, :], e_stats[:, 0, :])
                c.link(nc.vector.bn_aggr(e_mom[:, 1, :], e_stats[:, 1, :]))
                c.close()
                tt(e_mean[:, :], e_mom[:, 0, 0:1], e_mom[:, 1, 0:1], ALU.add)
                stt(e_var[:, :], e_mom[:, 0, 1:2], EDGE_EPS, e_mom[:, 1, 1:2], ALU.add, ALU.add).then_inc(s3_var, 1)

            def column_terms(b):
                c = Chain(dve, s3_cchain, 1, b)
                wait(dve, s3_rstd, b + 1)
                wait(dve, s3_qc, b + 1)
                c.link(ts(c_norm[:, :], C0[:, 0:NT], e_mean[:, :], e_rstd[:, :], ALU.subtract, ALU.mult))
                c.close()
                ts(c_one[:, :], c_norm[:, :], 1.0, None, ALU.add).then_inc(s3_c, 1)

            def edge_scores(b, j):
                wait(dve, s3_z, b * NT + j + 1)
                carry(6 + j)
                nc.vector.tensor_tensor_reduce(edge[:, j, :], scaled[:, j % 2], adjT[:, j, :], 1.0, -3.0e38,
                                               ALU.mult, ALU.max, col_max[:, j:j + 1]).then_inc(s3_e, 1)

            def column_shifts(b):
                c = Chain(dve, s3_mchain, 1, b)
                wait(dve, s3_e, b * NT + NT)
                c.link(ts(col_neg[:, :], col_max[:, :], -1.0, None, ALU.mult))
                c.close()
                stt(col_shift[:, :], col_max[:, :], -SLOPE, col_neg[:, :], ALU.mult, ALU.min).then_inc(s3_cm, 1)

            def leaky(b, j):
                wait(dve, s3_e, b * NT + j + 1)
                stt(edge[:, j, :], edge[:, j, :], SLOPE, edge[:, j, :], ALU.mult, ALU.max).then_inc(s3_l, 1)

            def column_inverse(b):
                wait(dve, s3_E, b * NT + NT)
                nc.vector.reciprocal(col_inv[:, :], col_sum[:, :]).then_inc(s3_inv, 1)

            def sigmoid_residual(b):
                wait(dve, s3_oN, b + 1)
                wait(dve, s_ln[3], b)
                tt(x4pre[:, :, :], tiles(C1), x3N[:, :, :], ALU.add).then_inc(s3_free, 1)

            ticks(dve, ((shifts, 1), (y2_residual, 3), (moments_of, 3, 2), (probabilities, 1, 0),
                  (sigmoid_residual, 4), (probabilities, 1, 1), (normalise, 3, 2),
                  (probabilities, 1, 2), (probabilities, 1, 3), (moments_of, 4, 3), (moments_of, 0, 0),
                  (pair_moments, 3), (normalise, 4, 3), (column_terms, 3), (edge_scores, 3, 0),
                  (row_inverse, 1), (edge_scores, 3, 1), (edge_scores, 3, 2), (edge_scores, 3, 3),
                  (leaky, 3, 0), (column_shifts, 3), (leaky, 3, 1), (leaky, 3, 2), (elu_residual, 1),
                  (leaky, 3, 3), (normalise, 0, 0), (moments_of, 1, 1), (y0_residual, 2),
                  (column_inverse, 3), (normalise, 1, 1), (scores, 0)))

        @block.gpsimd
        def _(pool):
            pool.wait_ge(s3_free, 1)

            def root(b, i):
                wait(pool, s_ln_var[i], b + 1)
                nc.gpsimd.tensor_tensor(rstd[i][:, :], var_eps[i][:, :], minus_half[:, :], ALU.pow).then_inc(s_ln_rstd[i], 1)

            def pair_root(b):
                wait(pool, s3_var, b + 1)
                nc.gpsimd.tensor_tensor(e_rstd[:, :], e_var[:, :], minus_half[:, 0:1], ALU.pow).then_inc(s3_rstd, 1)

            def x2_low(b):
                wait(pool, s2_hi, b + 1)
                nc.gpsimd.tensor_tensor(x2N_lo, x2N[:, :, :], x2N_hi.bitcast(F32), ALU.subtract).then_inc(s2_lo, 1)

            ticks(pool, ((x2_low, 2), (root, 3, 2), (root, 4, 3), (pair_root, 3), (root, 0, 0), (root, 1, 1)))


def kernel(x, adj, L0_gnn_w3_w, L0_gnn_w3_b, L0_gnn_u3_w, L0_gnn_u3_b, L0_gnn_w4_w, L0_gnn_w4_b, L0_gnn_w5_w,
           L0_gnn_w5_b, L0_gnn_u5_w, L0_gnn_u5_b, L1_gnn_W, L1_gnn_a_src, L1_gnn_a_dst, L2_gnn_weight_1, L3_gnn_a):
    import numpy as np
    import concourse.bacc as bacc
    from concourse.bass_utils import run_bass_kernel_spmd

    x = np.asarray(x)
    B, N, D = x.shape
    NT = N // P

    def nodes_first(a):
        return np.asarray(a).reshape(NT, P, -1).transpose(1, 0, 2)

    def halves(a):
        return np.asarray(a).reshape(D, 2, D).transpose(2, 1, 0).reshape(D, 2 * D)

    def col(a):
        return np.asarray(a).reshape(D, -1)

    a = np.asarray(L3_gnn_a)
    keep = dict(u3T=np.asarray(L0_gnn_u3_w).T, w_gat=np.asarray(L1_gnn_W), ident=np.eye(P, dtype=np.float32),
                a_src=col(L1_gnn_a_src), a_dst=col(L1_gnn_a_dst), a_i=a[:D], a_j=a[D:], w3_b=col(L0_gnn_w3_b),
                u3_b=col(L0_gnn_u3_b), w4_b=col(L0_gnn_w4_b), w5_b=col(L0_gnn_w5_b), u5_b=col(L0_gnn_u5_b),
                u5T=np.asarray(L0_gnn_u5_w).T)
    temp = dict(w3T=halves(L0_gnn_w3_w), w4T=halves(L0_gnn_w4_w), w5T=halves(L0_gnn_w5_w),
                cheb=np.asarray(L2_gnn_weight_1).transpose(0, 2, 1).reshape(D, -1), w_gatT=np.asarray(L1_gnn_W).T)
    arrays = dict(
        x_nat=x.reshape(B, NT, P, D).transpose(2, 0, 1, 3),
        x_tr=x.transpose(2, 0, 1),
        adj_nat=nodes_first(adj),
        adj_tr=nodes_first(np.asarray(adj).T),
        keep_pack=np.concatenate([keep[n] for n in KEEP], axis=1),
        temp_pack=np.concatenate([temp[n] for n in TEMP], axis=1),
    )
    arrays = {n: np.ascontiguousarray(v) for n, v in arrays.items()}
    nc = bacc.Bacc("TRN2", target_bir_lowering=False, num_devices=1)
    aps = {n: nc.dram_tensor(n, v.shape, F32, kind="ExternalInput").ap() for n, v in arrays.items()}
    aps["out"] = nc.dram_tensor("out", (P, B, NT, D), F32, kind="ExternalOutput").ap()
    build(nc, **aps)
    got = run_bass_kernel_spmd(nc, [arrays], core_ids=[0]).results[0]["out"]
    return np.ascontiguousarray(np.asarray(got).reshape(P, B, NT, D).transpose(1, 2, 0, 3).reshape(B, N, D))
```

```python
from contextlib import ExitStack

import concourse.bass as bass
from concourse import mybir

F32 = mybir.dt.float32
F32R = mybir.dt.float32r
ALU = mybir.AluOpType
ACT = mybir.ActivationFunctionType

P = 128
LN_EPS = 1e-5
EDGE_EPS = 1e-14
SLOPE = 0.2
MASKED = -(2.0**100)

KEEP = dict(u3T=(0, 128), w_gat=(128, 256), ident=(256, 384), a_src=(384, 385), a_dst=(385, 386),
            a_i=(386, 387), a_j=(387, 388), w3_b=(388, 389), u3_b=(389, 390), w4_b=(390, 391),
            w5_b=(391, 392), u5_b=(392, 393), u5T=(393, 521))
TEMP = dict(w3T=(0, 256), w4T=(256, 512), w5T=(512, 768), cheb=(768, 1664), w_gatT=(1664, 1792))


def wait(eng, sem, value):
    if not (isinstance(value, int) and value <= 0):
        eng.wait_ge(sem, value)


class Chain:

    def __init__(self, eng, sem, per, at):
        self.eng, self.sem, self.per, self.at, self.n = eng, sem, per, at, 0

    def link(self, instruction):
        self.n += 1
        instruction.then_inc(self.sem, 1)
        self.eng.wait_ge(self.sem, self.at * self.per + self.n)

    def close(self):
        assert self.n == self.per


def build(nc, x_nat, x_tr, adj_nat, adj_tr, keep_pack, temp_pack, out):
    _, B, NT, D = x_nat.shape
    N = NT * P
    S = 4
    STEPS = 5
    GROUPS = B // S
    assert D == P and B % S == 0

    with ExitStack() as ctx:
        def sb(name, shape, dt=F32):
            return ctx.enter_context(nc.sbuf_tensor(name, [P, *shape], dt))

        def sem(name):
            return ctx.enter_context(nc.semaphore(name))

        x_all = sb("x_all", [B, NT, D])
        adjT = sb("adjT", [NT, N])
        adjT_hi = sb("adjT_hi", [NT, N], F32R)
        adjT_lo = sb("adjT_lo", [NT, N], F32R)
        adj2T = sb("adj2T", [NT, N])
        mask = sb("mask", [NT, N])
        keep = sb("keep", [521])
        k = {n: keep[:, a:b] for n, (a, b) in KEEP.items()}
        ident = k["ident"]
        w3_hi, w3_lo = sb("w3_hi", [D], F32R), sb("w3_lo", [D], F32R)
        w43_hi, w43_lo = sb("w43_hi", [D], F32R), sb("w43_lo", [D], F32R)
        w5_hi, w5_lo = sb("w5_hi", [D], F32R), sb("w5_lo", [D], F32R)
        u3_hi, u3_lo = sb("u3_hi", [D], F32R), sb("u3_lo", [D], F32R)
        u5_hi, u5_lo = sb("u5_hi", [D], F32R), sb("u5_lo", [D], F32R)
        u5h = sb("u5h", [D])
        bias_z, bias_r, bias_h = sb("bias_z", [1]), sb("bias_r", [1]), sb("bias_h", [1])
        w_cheb = sb("w_cheb", [4 * D])
        w_x, w_u = w_cheb[:, 0:2 * D], w_cheb[:, 2 * D:4 * D]
        wa_src_row, a_j_row = sb("wa_src_row", [D]), sb("a_j_row", [D])
        wa_dst_rows = sb("wa_dst_rows", [D])
        a_i_rows, a_j_rows = sb("a_i_rows", [D]), sb("a_j_rows", [D])
        a_ij_rows, halves = sb("a_ij_rows", [D]), sb("halves", [P])
        a_src_rows, a_dst_rows = sb("a_src_rows", [D]), sb("a_dst_rows", [D])
        minus_half = sb("minus_half", [NT])
        carrier = sb("carrier", [12])
        w_sum = sb("w_sum", [3 * D])

        state = sb("state", [S, N])
        hT = [state[:, s, :] for s in range(S)]
        prob = state
        work = sb("work", [10, N])
        tz, tr, rh = work[:, 0:2, :], work[:, 2:4, :], work[:, 4:6, :]
        th, dh = work[:, 6:8, :], work[:, 8:10, :]
        probT = work[:, 0:4, :]
        e_hi, e_lo = work[:, 4:6, :], work[:, 6:8, :]
        temp = work[:, 0:4, :].rearrange("p a n -> p (a n)")
        w = {n: temp[:, a:b] for n, (a, b) in TEMP.items()}
        hN = sb("hN", [S, 2, NT, D], F32R)
        x2N_hi, x2N_lo = hN[:, 0, 0], hN[:, 0, 1]
        mT_hi, mT_lo = sb("mT_hi", [2, N], F32R), sb("mT_lo", [2, N], F32R)
        parts = sb("parts", [8, N], F32R)
        hT_hi, hT_lo, rh_hi, rh_lo = (parts[:, i:i + 2] for i in (0, 2, 4, 6))

        edge = sb("edge", [NT, N])
        x1N, x1T, gatN = sb("x1N", [NT, D]), sb("x1T", [N]), sb("gatN", [NT, D])
        ex, rl, x2pre = sb("ex", [NT, D]), sb("rl", [NT, D]), sb("x2pre", [NT, D])
        x2T, uT, gN = sb("x2T", [N]), sb("uT", [N]), sb("gN", [NT, D])
        x2N, x3pre = sb("x2N", [NT, D]), sb("x3pre", [NT, D])
        x3N, x3T, scaled = sb("x3N", [NT, D]), sb("x3T", [N]), sb("scaled", [2, N])
        yN, sgN, x4pre = sb("yN", [NT, D]), sb("sgN", [NT, D]), sb("x4pre", [NT, D])
        BY_SCALAR = (3,)
        stats = [sb(f"stats{i}", [NT, 6]) for i in range(4)]
        moments = [sb(f"moments{i}", [NT, 2]) for i in range(4)]
        var_eps = [sb(f"var_eps{i}", [NT]) for i in range(4)]
        rstd = [sb(f"rstd{i}", [NT]) for i in range(4)]
        centre = {i: sb(f"centre{i}", [NT]) for i in BY_SCALAR}
        row_max, s_max, s_leak, shift = (sb(n, [NT]) for n in ("row_max", "s_max", "s_leak", "shift"))
        bias_1, bias_s, row_sum, row_inv = (sb(n, [NT]) for n in ("bias_1", "bias_s", "row_sum", "row_inv"))
        e_stats, e_mom = sb("e_stats", [6]), sb("e_mom", [2])
        e_mean, e_var, e_rstd = sb("e_mean", [1]), sb("e_var", [1]), sb("e_rstd", [1])
        c_norm, c_one = sb("c_norm", [NT]), sb("c_one", [NT])
        col_max, col_neg, col_shift = sb("col_max", [NT]), sb("col_neg", [NT]), sb("col_shift", [NT])
        own, q_cols, product = sb("own", [NT]), sb("q_cols", [NT]), sb("product", [2, NT, D])
        col_sum, col_inv = sb("col_sum", [NT]), sb("col_inv", [NT])

        bank = [ctx.enter_context(nc.psum_tensor(f"bank{i}", [P, N], F32)) for i in range(8)]
        ps_m, ps_zr, ps_h, ps_t = bank[0:2], bank[2:4], bank[4:6], bank[6:8]
        A0, A1, A2, B0, B1, B2, C0, C1 = bank

        def tiles(b):
            return b[:, :].rearrange("p (t d) -> p t d", t=NT)

        def sems(names):
            return [sem(n) for n in names.split()]

        (keep_loaded, gate_weights_loaded, temp_loaded, adjN_loaded, x_0_loaded, x_first_loaded,
         x_rest_loaded, stored, x1_moved) = sems(
            "keep_loaded gate_weights_loaded temp_loaded adjN_loaded x_0_loaded x_first_loaded "
            "x_rest_loaded stored x1_moved")
        adjT_loaded = [sem("adjT_loaded0"), sem("adjT_loaded1")]
        state_loaded = [sem(f"state_loaded{s}") for s in range(S)]
        (biases_ready, rows_ready, folded_ready, folded_copied, weights_step, adj_hi_ready,
         adj_lo_ready, adj2_ready, adj2_copied, mask_step) = sems(
            "biases_ready rows_ready folded_ready folded_copied weights_step adj_hi_ready "
            "adj_lo_ready adj2_ready adj2_copied mask_step")
        (m_ready, m_hi_ready, m_lo_ready, h_hi_ready, h_lo_ready, z_ready, tz_ready, r_ready,
         tr_ready, rh_ready, rh_hi_ready, rh_lo_ready, candidate_ready, th_ready, dh_ready,
         step_ready, h_ready, h_turned, hN_hi_ready, hN_lo_ready) = sems(
            "m_ready m_hi_ready m_lo_ready h_hi_ready h_lo_ready z_ready tz_ready r_ready tr_ready "
            "rh_ready rh_hi_ready rh_lo_ready candidate_ready th_ready dh_ready step_ready h_ready "
            "h_turned hN_hi_ready hN_lo_ready")
        norm_done, norm_chain, var_ready, rstd_ready = (
            [sem(f"{n}{i}") for i in range(4)] for n in ("norm_done", "norm_chain", "var_ready", "rstd_ready"))
        centre_ready = {i: sem(f"centre_ready{i}") for i in BY_SCALAR}
        x1_done = norm_done[0]
        (shift_chain, x1_turned, x1_copied, projection_ready, projection_copied, near_ready,
         own_ready, scores_ready, shifts_ready, exps_ready, probs_ready, probs_turned,
         probs_copied, attended_ready, row_inv_ready, elu_exp_ready, elu_relu_ready, elu_ready,
         x2pre_ready) = sems(
            "shift_chain x1_turned x1_copied projection_ready projection_copied near_ready own_ready "
            "scores_ready shifts_ready exps_ready probs_ready probs_turned probs_copied "
            "attended_ready row_inv_ready elu_exp_ready elu_relu_ready elu_ready x2pre_ready")
        (x2_hi_ready, x2_lo_ready, x2_turned, x2_copied, u_ready, u_copied, g_ready, g_copied,
         y_ready, x3pre_ready) = sems(
            "x2_hi_ready x2_lo_ready x2_turned x2_copied u_ready u_copied g_ready g_copied y_ready "
            "x3pre_ready")
        (pair_moments_ready, columns_chain, maxima_chain, x3_turned, x3_copied, p_ready, pq_ready,
         pair_stats_ready, q_cols_ready, pair_sums_ready, pair_var_ready, pair_rstd_ready,
         columns_ready, normed_ready, edge_scores_ready, column_shift_ready, leaky_ready,
         edge_exps_ready, column_inv_ready, shares_ready, gathered_ready, tanh_ready,
         sigmoid_ready, x4pre_ready) = sems(
            "pair_moments_ready columns_chain maxima_chain x3_turned x3_copied p_ready pq_ready "
            "pair_stats_ready q_cols_ready pair_sums_ready pair_var_ready pair_rstd_ready "
            "columns_ready normed_ready edge_scores_ready column_shift_ready leaky_ready "
            "edge_exps_ready column_inv_ready shares_ready gathered_ready tanh_ready sigmoid_ready "
            "x4pre_ready")

        SLOTS = B * STEPS

        def one(b):
            return x_all[:, bass.ds(b, 1)].rearrange("p a t d -> p (a t) d")

        class Slot:
            def __init__(self, q, s, group, step, last, final):
                self.q, self.s, self.i, self.group, self.step = q, s, s % 2, group, step
                self.last, self.final = last, final

            def graph(self, later=0):
                return one(self.group * S + self.s + later)

        def slots(eng, stages):
            def one_step(step, group, last=False, final=False):
                for m in range(S):
                    for stage, lead in stages:
                        q = group * (STEPS * S) + step * S + m + lead
                        if isinstance(q, int) and not 0 <= q < SLOTS:
                            continue
                        ahead = last and m + lead >= S
                        stage(Slot(q, (m + lead) % S, group + 1 if ahead else group, step, last, final))

            def group_steps(group, final=False):
                with eng.Fori(0, STEPS - 1, 1) as step:
                    one_step(step, group)
                one_step(STEPS - 1, group, last=True, final=final)

            one_step(-1, 0)
            group_steps(0)
            with eng.Fori(1, GROUPS - 1, 1) as group:
                group_steps(group)
            group_steps(GROUPS - 1, final=True)

        LAG = 4

        def ticks(eng, order):
            def tick(t):
                for stage, lag, *args in order:
                    b = t - lag
                    if not isinstance(b, int) or 0 <= b < B:
                        stage(b, *args)
            for t in range(LAG + 1):
                tick(t)
            with eng.Fori(LAG + 1, B, 1) as t:
                tick(t)
            for t in range(B, B + LAG):
                tick(t)

        block = ctx.enter_context(nc.Block())

        @block.sync
        def _(sp):
            sp.dma_start(x_all[:, 0:1], x_nat[:, 0:1]).then_inc(x_0_loaded, 16)
            for half in range(2):
                two = slice(2 * half, 2 * half + 2)
                sp.dma_start(adjT[:, two, :], adj_tr[:, two, :]).then_inc(adjT_loaded[half], 16)
            sp.dma_start(keep[:, :], keep_pack).then_inc(keep_loaded, 16)
            gates_end, end = TEMP["w5T"][1], TEMP["w_gatT"][1]
            sp.dma_start(temp[:, 0:gates_end], temp_pack[:, 0:gates_end]).then_inc(gate_weights_loaded, 16)
            sp.dma_start(hT[0], x_tr[:, 0, :]).then_inc(state_loaded[0], 16)
            sp.dma_start(x_all[:, 1:S], x_nat[:, 1:S]).then_inc(x_first_loaded, 16)
            sp.dma_start(temp[:, gates_end:end], temp_pack[:, gates_end:end]).then_inc(temp_loaded, 16)
            for s in range(1, S):
                sp.dma_start(hT[s], x_tr[:, s, :]).then_inc(state_loaded[s], 16)
            sp.dma_start(edge[:, :, :], adj_nat).then_inc(adjN_loaded, 16)
            for g in range(1, GROUPS):
                sp.dma_start(x_all[:, g * S:(g + 1) * S],
                        x_nat[:, g * S:(g + 1) * S]).then_inc(x_rest_loaded, 16)
            with sp.Fori(1, GROUPS, 1) as g:
                for s in range(S):
                    sp.wait_ge(h_turned, g * (STEPS * S) - S + s + 1)
                    sp.dma_start(hT[s],
                            x_tr[:, bass.ds(g * S + s, 1), :].rearrange("p a n -> p (a n)")).then_inc(state_loaded[s], 16)

            def bring(b):
                sp.wait_ge(x1_done, b + 2)
                wait(sp, x1_turned, b)
                wait(sp, own_ready, b)
                sp.dma_start(x1N[:, :, :], one(b)).then_inc(x1_moved, 16)

            def store(b):
                sp.wait_ge(norm_done[3], b + 1)
                sp.dma_start(out[:, bass.ds(b, 1)], x_all[:, bass.ds(b, 1)]).then_inc(stored, 16)

            for b in range(LAG + 1):
                bring(b)
            with sp.Fori(LAG + 1, B, 1) as b:
                bring(b)
                store(b - LAG - 1)
            with sp.Fori(B - LAG - 1, B, 1) as b:
                store(b)
            sp.wait_ge(stored, 16 * B)

        @block.tensor
        def _(pe):
            mm = nc.tensor.matmul

            def split_mm(psum, wt, mv, start, stop):
                (wt_hi, wt_lo), (mv_hi, mv_lo) = wt, mv
                mm(psum, wt_hi, mv_hi, start=start, stop=False, skip_group_check=True)
                mm(psum, wt_lo, mv_hi, start=False, stop=False, skip_group_check=True)
                return mm(psum, wt_hi, mv_lo, start=False, stop=stop, skip_group_check=True)

            def by_adj(psum, xN_hi, xN_lo, aT_hi, aT_lo):
                for j in range(NT):
                    mm(psum, xN_hi[:, j, :], aT_hi[:, j, :], start=(j == 0), stop=False)
                    mm(psum, xN_hi[:, j, :], aT_lo[:, j, :], start=False, stop=False)
                for j in range(NT):
                    last = mm(psum, xN_lo[:, j, :], aT_hi[:, j, :], start=False, stop=(j == NT - 1))
                return last

            def transposes(psum, src):
                for t in range(NT):
                    last = nc.tensor.transpose(psum[:, t * P:(t + 1) * P], src[:, t * P:(t + 1) * P], ident)
                return last

            def fold_attention():
                pe.wait_ge(temp_loaded, 16)
                pe.wait_ge(rows_ready, 1)
                mm(bank[5][:, 0:D], a_src_rows[:, :], w["w_gatT"], start=True, stop=True)
                mm(bank[6][:, 0:D], a_j_rows[:, :], ident, start=True, stop=True)
                mm(bank[7][:, 0:D], w["w_gatT"], a_dst_rows[:, :], start=True,
                        stop=True).then_inc(folded_ready, 1)

            pe.wait_ge(adj_hi_ready, 2)
            pe.wait_ge(adj_lo_ready, 2)

            def messages(slot):
                i = slot.i
                wait(pe, hN_hi_ready, slot.q + 1)
                wait(pe, hN_lo_ready, slot.q + 1)
                by_adj(ps_m[i][:, :], hN[:, slot.s, 0], hN[:, slot.s, 1], adjT_hi, adjT_lo).then_inc(m_ready, 1)

            def state_part(slot):
                i = slot.i
                if isinstance(slot.q, int) and slot.q == 0:
                    fold_attention()
                    pe.wait_ge(weights_step, 4)
                wait(pe, h_hi_ready, slot.q + 1)
                wait(pe, h_lo_ready, slot.q + 1)
                split_mm(ps_zr[i][:, :], (u3_hi[:, :], u3_lo[:, :]), (hT_hi[:, i], hT_lo[:, i]), True, False)

            def z_sum(slot):
                i = slot.i
                if isinstance(slot.q, int) and slot.q == 0:
                    pe.wait_ge(folded_copied, 1)
                wait(pe, m_hi_ready, slot.q + 1)
                wait(pe, m_lo_ready, slot.q + 1)
                split_mm(ps_zr[i][:, :], (w3_hi[:, :], w3_lo[:, :]), (mT_hi[:, i], mT_lo[:, i]), False,
                        True).then_inc(z_ready, 1)

            def candidate_part(slot):
                i = slot.i
                split_mm(ps_h[i][:, :], (w5_hi[:, :], w5_lo[:, :]), (mT_hi[:, i], mT_lo[:, i]), True, False)

            def r_sum(slot):
                i = slot.i
                wait(pe, tz_ready, slot.q + 1)
                split_mm(ps_zr[i][:, :], (w43_hi[:, :], w43_lo[:, :]), (mT_hi[:, i], mT_lo[:, i]), False,
                        True).then_inc(r_ready, 1)

            def candidate_sum(slot):
                i = slot.i
                wait(pe, rh_hi_ready, slot.q + 1)
                wait(pe, rh_lo_ready, slot.q + 1)
                split_mm(ps_h[i][:, :], (u5_hi[:, :], u5_lo[:, :]), (rh_hi[:, i], rh_lo[:, i]), False,
                        True).then_inc(candidate_ready, 1)

            def to_natural(slot):
                i = slot.i
                wait(pe, h_ready, slot.q + 1)
                wait(pe, hN_lo_ready, S + slot.q - 1)
                if not (slot.final and slot.s >= 2):
                    wait(pe, hN_hi_ready, S + slot.q - 1)
                transposes(ps_t[i], hT[slot.s]).then_inc(h_turned, 1)

            slots(pe, ((messages, 3), (to_natural, 0), (z_sum, 2), (candidate_sum, 1), (candidate_part, 2),
                       (state_part, 3), (r_sum, 2)))

            def adj_square(b):
                for j in (2 * b, 2 * b + 1) if isinstance(b, int) and b < 2 else ():
                    if j == 0:
                        pe.wait_ge(adjN_loaded, 16)
                        pe.wait_ge(hN_lo_ready, SLOTS + S)
                    if j >= 2:
                        pe.wait_ge(adj2_copied, j - 1)
                    for q in range(NT):
                        last = mm((C0, C1)[j % 2][:, :], edge[:, q, j * P:(j + 1) * P], adjT[:, q, :],
                                  start=(q == 0), stop=(q == NT - 1))
                    last.then_inc(adj2_ready, 1)

            def flat_(x):
                return x[:, :, :].rearrange("p t d -> p (t d)")

            def x1_turn(b):
                wait(pe, x1_moved, 16 * b + 16)
                wait(pe, probs_copied, b * NT)
                transposes(A2, flat_(x1N)).then_inc(x1_turned, 1)

            def near_row(b):
                wait(pe, x1_copied, b + 1)
                mm(A2[:, :], wa_dst_rows[:, :], x1T[:, :], start=True, stop=True).then_inc(near_ready, 1)

            def project(b):
                wait(pe, x1_copied, b + 1)
                for t in range(NT):
                    last = mm(A1[:, t * D:(t + 1) * D], x1T[:, t * P:(t + 1) * P], k["w_gat"], start=True,
                            stop=True)
                last.then_inc(projection_ready, 1)

            def prob_turn(j):
                for t in range(NT):
                    last = nc.tensor.transpose((A0, A2, A1, A2)[j][:, t * P:(t + 1) * P],
                                               prob[:, t, j * P:(j + 1) * P], ident)
                last.then_inc(probs_turned, 1)

            def prob_turns(b):
                wait(pe, probs_ready, b * NT + NT)
                wait(pe, elu_exp_ready, b)
                wait(pe, elu_relu_ready, b)
                prob_turn(0)
                prob_turn(1)

            def prob_turn_2(b):
                wait(pe, projection_copied, b + 1)
                prob_turn(2)

            def prob_turn_3(b):
                wait(pe, probs_copied, b * NT + 2)
                prob_turn(3)

            def attend(b, i):
                if i == 0:
                    wait(pe, probs_copied, b * NT + NT)
                for j in range(NT):
                    last = mm(A0[:, i * D:(i + 1) * D], probT[:, j, i * P:(i + 1) * P], gatN[:, j, :],
                              start=(j == 0), stop=(j == NT - 1))
                if i == NT - 1:
                    last.then_inc(attended_ready, 1)

            def x2_turn(b):
                wait(pe, norm_done[1], b + 1)
                transposes(B0, flat_(x2N)).then_inc(x2_turned, 1)

            def once(b):
                wait(pe, x2_hi_ready, b + 1)
                wait(pe, x2_lo_ready, b + 1)
                wait(pe, x3_copied, b)
                by_adj(B1[:, :], x2N_hi, x2N_lo, adjT_hi, adjT_lo).then_inc(u_ready, 1)

            def weigh(b):
                wait(pe, x2_copied, b + 1)
                wait(pe, u_copied, b + 1)
                for t in range(NT):
                    psum = (B2, B0)[t // 2][:, (t % 2) * 2 * D:(t % 2 + 1) * 2 * D]
                    mm(psum, x2T[:, t * P:(t + 1) * P], w_x, start=(t % 2 == 0), stop=False,
                            skip_group_check=True)
                    last = mm(psum, uT[:, t * P:(t + 1) * P], w_u, start=False, stop=True,
                            skip_group_check=True)
                last.then_inc(g_ready, 1)

            def twice(b):
                wait(pe, g_copied, b + 1)
                if isinstance(b, int) and b == 0:
                    pe.wait_ge(adj2_copied, NT)
                for t in range(NT):
                    psum = (B2, B0)[t // 2][:, (t % 2) * 2 * D + D:(t % 2 + 1) * 2 * D]
                    for j in range(NT):
                        last = mm(psum, adj2T[:, j, t * P:(t + 1) * P], gN[:, j, :], start=False,
                                stop=(j == NT - 1),
                                  skip_group_check=True)
                last.then_inc(y_ready, 1)

            def x3_turn(b):
                wait(pe, norm_done[2], b + 1)
                transposes(B1, flat_(x3N)).then_inc(x3_turned, 1)

            def pair_mixed(b):
                wait(pe, x3_copied, b + 1)
                wait(pe, tanh_ready, b)
                mm(C0[:, :], a_ij_rows[:, :], x3T[:, :], start=True, stop=True).then_inc(pq_ready, 1)

            def pair_row(b):
                wait(pe, x3_copied, b + 1)
                wait(pe, normed_ready, b * NT)
                mm(C1[:, :], a_i_rows[:, :], x3T[:, :], start=True, stop=True).then_inc(p_ready, 1)

            def pair_sums(b):
                wait(pe, pair_moments_ready, b + 1)
                mm(C0[:, 0:2], halves[:, :], e_mom[:, :], start=True, stop=True).then_inc(pair_sums_ready, 1)

            def gather(b):
                wait(pe, shares_ready, b + 1)
                for i in range(NT):
                    for j in range(NT):
                        last = mm(C0[:, i * D:(i + 1) * D], edge[:, j, i * P:(i + 1) * P], yN[:, j, :],
                                  start=(j == 0), stop=(j == NT - 1))
                last.then_inc(gathered_ready, 1)

            ticks(pe, ((twice, 3), (x1_turn, 0), (attend, 1, 0), (near_row, 0), (gather, 4), (attend, 1, 1),
                  (attend, 1, 2), (attend, 1, 3), (x2_turn, 2), (x3_turn, 3), (project, 0),
                  (adj_square, 0), (pair_mixed, 3), (once, 2), (pair_sums, 3), (pair_row, 3),
                  (prob_turns, 0), (weigh, 2), (prob_turn_2, 0), (prob_turn_3, 0)))

        @block.scalar
        def _(act):
            def copy(dst, src):
                return nc.scalar.activation(dst, src, ACT.Copy)

            act.wait_ge(x_0_loaded, 16)
            copy(hN[:, 0, 0], x_all[:, 0]).then_inc(hN_hi_ready, 1)
            for half in range(2):
                two = slice(2 * half, 2 * half + 2)
                act.wait_ge(adjT_loaded[half], 16)
                copy(adjT_hi[:, two, :], adjT[:, two, :]).then_inc(adj_hi_ready, 1)
            act.wait_ge(x_first_loaded, 16)
            for s in range(1, S):
                copy(hN[:, s, 0], x_all[:, s]).then_inc(hN_hi_ready, 1)
            act.wait_ge(biases_ready, 1)

            def state_high(slot):
                i = slot.i
                wait(act, state_loaded[slot.s], 16 * slot.group + 16)
                copy(hT_hi[:, i], hT[slot.s]).then_inc(h_hi_ready, 1)

            def message_high(slot):
                i = slot.i
                wait(act, m_ready, slot.q + 1)
                copy(mT_hi[:, i], ps_m[i][:, :]).then_inc(m_hi_ready, 1)

            def z_tanh(slot):
                i = slot.i
                wait(act, z_ready, slot.q + 1)
                nc.scalar.activation(tz[:, i], ps_zr[i][:, :], ACT.Tanh, bias=bias_z[:, :],
                                     scale=0.5).then_inc(tz_ready, 1)

            def r_tanh(slot):
                i = slot.i
                wait(act, r_ready, slot.q + 1)
                nc.scalar.activation(tr[:, i], ps_zr[i][:, :], ACT.Tanh, bias=bias_r[:, :],
                                     scale=0.5).then_inc(tr_ready, 1)

            def reset_high(slot):
                i = slot.i
                wait(act, rh_ready, slot.q + 1)
                copy(rh_hi[:, i], rh[:, i]).then_inc(rh_hi_ready, 1)

            def candidate_tanh(slot):
                i = slot.i
                wait(act, candidate_ready, slot.q + 1)
                nc.scalar.activation(th[:, i], ps_h[i][:, :], ACT.Tanh, bias=bias_h[:, :]).then_inc(th_ready, 1)

            def natural_high(slot):
                i = slot.i
                if not slot.last:
                    wait(act, h_turned, slot.q + 1)
                    copy(hN[:, slot.s, 0], tiles(ps_t[i])).then_inc(hN_hi_ready, 1)
                elif not slot.final:
                    wait(act, m_ready, slot.q + 1)
                    act.wait_ge(x_rest_loaded, 16 * (GROUPS - 1))
                    copy(hN[:, slot.s, 0], slot.graph(S)).then_inc(hN_hi_ready, 1)

            slots(act, ((r_tanh, 1), (state_high, 3), (reset_high, 1), (message_high, 3), (natural_high, 0),
                        (z_tanh, 2), (candidate_tanh, 1)))

            def adj2_rows(b):
                for j in (2 * b, 2 * b + 1) if isinstance(b, int) and b < 2 else ():
                    act.wait_ge(adj2_ready, j + 1)
                    copy(adj2T[:, j, :], (C0, C1)[j % 2][:, :]).then_inc(adj2_copied, 1)

            def normalise(b, i):
                wait(act, centre_ready[i], b + 1)
                for t in range(NT):
                    last = nc.scalar.activation(one(b)[:, t, :], x4pre[:, t, :], ACT.Identity,
                            bias=centre[i][:, t:t + 1],
                                                scale=rstd[i][:, t:t + 1])
                last.then_inc(norm_done[i], 1)

            def x1_cols(b):
                wait(act, x1_turned, b + 1)
                copy(x1T[:, :], A2[:, :]).then_inc(x1_copied, 1)

            def projected(b):
                wait(act, projection_ready, b + 1)
                copy(gatN[:, :, :], tiles(A1)).then_inc(projection_copied, 1)

            def line_exps(b, t):
                if t == 0:
                    wait(act, shifts_ready, b + 1)
                if t >= 2:
                    wait(act, probs_ready, b * NT + t - 1)
                nc.scalar.activation(e_hi[:, t % 2], state[:, t, :], ACT.Exp, bias=bias_1[:, t:t + 1])
                nc.scalar.activation(e_lo[:, t % 2], state[:, t, :], ACT.Exp, bias=bias_s[:, t:t + 1],
                                     scale=SLOPE).then_inc(exps_ready, 1)

            def prob_cols(b, j):
                wait(act, probs_turned, b * NT + j + 1)
                copy(probT[:, j, :], (A0, A2, A1, A2)[j][:, :]).then_inc(probs_copied, 1)

            def elu_parts(b, func, dst, done):
                wait(act, row_inv_ready, b + 1)
                wait(act, attended_ready, b + 1)
                for t in range(NT):
                    last = nc.scalar.activation(dst[:, t, :], A0[:, t * D:(t + 1) * D], func,
                                                scale=row_inv[:, t:t + 1])
                last.then_inc(done, 1)

            def elu_exp(b):
                elu_parts(b, ACT.Exp, ex, elu_exp_ready)

            def elu_relu(b):
                elu_parts(b, ACT.Relu, rl, elu_relu_ready)

            def x2_high(b):
                wait(act, norm_done[1], b + 1)
                copy(x2N_hi, x2N[:, :, :]).then_inc(x2_hi_ready, 1)

            def x2_cols(b):
                wait(act, x2_turned, b + 1)
                copy(x2T[:, :], B0[:, :]).then_inc(x2_copied, 1)

            def u_cols(b):
                wait(act, u_ready, b + 1)
                copy(uT[:, :], B1[:, :]).then_inc(u_copied, 1)

            def g_rows(b):
                wait(act, g_ready, b + 1)
                wait(act, y_ready, b)
                for q, psum in enumerate((B2, B0)):
                    last = copy(gN[:, 2 * q:2 * q + 2, :],
                                psum[:, :].rearrange("p (t k d) -> p t k d", t=2, k=2)[:, :, 0, :])
                last.then_inc(g_copied, 1)

            def x3_cols(b):
                wait(act, x3_turned, b + 1)
                copy(x3T[:, :], B1[:, :]).then_inc(x3_copied, 1)

            def normed(b, j):
                if j == 0:
                    wait(act, p_ready, b + 1)
                    wait(act, columns_ready, b + 1)
                if j >= 2:
                    wait(act, edge_scores_ready, b * NT + j - 1)
                nc.scalar.activation(scaled[:, j % 2], C1[:, :], ACT.Identity, bias=c_one[:, j:j + 1],
                                     scale=e_rstd[:, :]).then_inc(normed_ready, 1)

            def edge_exp(b, j):
                if j == 0:
                    wait(act, column_shift_ready, b + 1)
                wait(act, leaky_ready, b * NT + j + 1)
                nc.scalar.activation(edge[:, j, :], edge[:, j, :], ACT.Exp, bias=col_shift[:, j:j + 1],
                                     accum_out=col_sum[:, j:j + 1]).then_inc(edge_exps_ready, 1)

            def shares(b):
                wait(act, column_inv_ready, b + 1)
                for j in range(NT):
                    last = nc.scalar.activation(yN[:, j, :], x3N[:, j, :], ACT.Copy, scale=col_inv[:, j:j + 1])
                last.then_inc(shares_ready, 1)

            def sigmoid(b):
                wait(act, gathered_ready, b + 1)
                wait(act, x4pre_ready, b + 1)
                nc.scalar.activation(sgN[:, :, :], tiles(C0), ACT.Tanh, scale=0.5).then_inc(tanh_ready, 1)
                wait(act, tanh_ready, b + 1)
                nc.scalar.activation(sgN[:, :, :], sgN[:, :, :], ACT.Copy, scale=0.5,
                        bias=0.5).then_inc(sigmoid_ready, 1)

            ticks(act, ((prob_cols, 1, 3), (edge_exp, 4, 2), (edge_exp, 4, 3), (x1_cols, 0), (shares, 4),
                   (x2_high, 2), (sigmoid, 4), (line_exps, 0, 0), (line_exps, 0, 1), (x3_cols, 3),
                   (line_exps, 0, 2), (elu_relu, 1), (line_exps, 0, 3), (adj2_rows, 0), (elu_exp, 1),
                   (x2_cols, 2), (u_cols, 2), (normed, 3, 0), (projected, 0), (normed, 3, 1),
                   (prob_cols, 0, 0), (normed, 3, 2), (normed, 3, 3), (prob_cols, 0, 1), (g_rows, 2),
                   (normalise, 4, 3), (edge_exp, 3, 0), (prob_cols, 0, 2), (edge_exp, 3, 1)))

        @block.vector
        def _(dve):
            tt, ts = nc.vector.tensor_tensor, nc.vector.tensor_scalar
            stt, cp = nc.vector.scalar_tensor_tensor, nc.vector.tensor_copy

            def rest(dst, whole, hi):
                return tt(dst, whole, hi.bitcast(F32), ALU.subtract)

            def carry(site):
                nc.vector.memset(carrier[:, site:site + 1], 0.0)

            nc.vector.memset(minus_half[:, :], -0.5).then_inc(x4pre_ready, 1)
            nc.vector.memset(carrier[:, :], 0.0).then_inc(x1_done, 1)
            dve.wait_ge(hN_hi_ready, 1)
            rest(hN[:, 0, 1], x_all[:, 0], hN[:, 0, 0]).then_inc(hN_lo_ready, 1)
            for half in range(2):
                two = slice(2 * half, 2 * half + 2)
                dve.wait_ge(adj_hi_ready, half + 1)
                rest(adjT_lo[:, two, :], adjT[:, two, :], adjT_hi[:, two, :]).then_inc(adj_lo_ready, 1)
            dve.wait_ge(keep_loaded, 16)

            def rows(dst, col):
                return ts(dst, ident, 0.0, col, ALU.mult, ALU.add)

            rows(a_src_rows[:, :], k["a_src"])
            rows(a_j_rows[:, :], k["a_j"])
            rows(a_dst_rows[:, :], k["a_dst"]).then_inc(rows_ready, 1)
            rows(a_i_rows[:, :], k["a_i"])
            ts(a_ij_rows[:, 0:P // 2], ident[:, 0:P // 2], 0.0, k["a_i"], ALU.mult, ALU.add)
            ts(a_ij_rows[:, P // 2:P], ident[:, P // 2:P], 0.0, k["a_j"], ALU.mult, ALU.add)
            nc.vector.memset(halves[:, :], 2.0 / P)
            dve.wait_ge(gate_weights_loaded, 16)
            tt(w_sum[:, 0:D], w["w3T"][:, 0:D], w["w3T"][:, D:2 * D], ALU.add)
            tt(w_sum[:, D:2 * D], w["w4T"][:, 0:D], w["w4T"][:, D:2 * D], ALU.add)
            tt(w_sum[:, 2 * D:3 * D], w["w5T"][:, 0:D], w["w5T"][:, D:2 * D], ALU.add)
            tt(bias_z[:, :], k["w3_b"], k["u3_b"], ALU.add)
            tt(bias_r[:, :], k["w4_b"], k["u3_b"], ALU.add)
            tt(bias_h[:, :], k["w5_b"], k["u5_b"], ALU.add).then_inc(weights_step, 1)
            dve.wait_ge(weights_step, 1)
            ts(u5h[:, :], k["u5T"], 0.5, None, ALU.mult)
            cp(u3_hi[:, :], k["u3T"])
            ts(bias_z[:, :], bias_z[:, :], 0.5, None, ALU.mult)
            ts(bias_r[:, :], bias_r[:, :], 0.5, None, ALU.mult).then_inc(biases_ready, 1)
            cp(w3_hi[:, :], w_sum[:, 0:D])
            cp(w5_hi[:, :], w_sum[:, 2 * D:3 * D])
            tt(w_sum[:, D:2 * D], w_sum[:, D:2 * D], w_sum[:, 0:D], ALU.subtract).then_inc(weights_step, 1)
            dve.wait_ge(weights_step, 2)
            cp(w43_hi[:, :], w_sum[:, D:2 * D])
            cp(u5_hi[:, :], u5h[:, :])
            rest(u3_lo[:, :], k["u3T"], u3_hi[:, :])
            rest(w3_lo[:, :], w_sum[:, 0:D], w3_hi[:, :])
            rest(w5_lo[:, :], w_sum[:, 2 * D:3 * D], w5_hi[:, :]).then_inc(weights_step, 1)
            dve.wait_ge(weights_step, 3)
            rest(u5_lo[:, :], u5h[:, :], u5_hi[:, :])
            rest(w43_lo[:, :], w_sum[:, D:2 * D], w43_hi[:, :]).then_inc(weights_step, 1)
            dve.wait_ge(temp_loaded, 16)
            cheb = w["cheb"].rearrange("p (k d) -> p k d", d=D)
            cp(w_cheb[:, D:2 * D], cheb[:, 0])
            for power, at in ((2, 0), (3, 2), (1, 3)):
                tt(w_cheb[:, at * D:(at + 1) * D], cheb[:, power], cheb[:, power + 3], ALU.add)
            for s in range(1, S):
                dve.wait_ge(hN_hi_ready, s + 1)
                rest(hN[:, s, 1], x_all[:, s], hN[:, s, 0]).then_inc(hN_lo_ready, 1)
            dve.wait_ge(folded_ready, 1)
            cp(wa_src_row[:, :], bank[5][:, 0:D])
            cp(a_j_row[:, :], bank[6][:, 0:D])
            cp(wa_dst_rows[:, :], bank[7][:, 0:D]).then_inc(folded_copied, 1)

            def tile_of(x):
                return lambda t: x[:, t, :]

            def ln_source(b, i):
                return (tile_of(one(b)), tile_of(x2pre), tile_of(x3pre), tile_of(x4pre))[i]

            def row_stats(b, i):
                wait(dve, norm_done[i], b + 1 if i == 0 else b)
                if i == 1:
                    wait(dve, x2pre_ready, b + 1)
                if i == 2:
                    wait(dve, x3pre_ready, b + 1)
                if i == 3:
                    wait(dve, x4pre_ready, b + 2)
                src = ln_source(b, i)
                for t in range(NT):
                    last = nc.vector.bn_stats(stats[i][:, t, :], src(t))
                last.then_inc(norm_chain[i], 1)

            def row_moments(b, i):
                wait(dve, norm_chain[i], 2 * b + 1)
                carry(i)
                for t in range(NT):
                    last = nc.vector.bn_aggr(moments[i][:, t, :], stats[i][:, t, :])
                last.then_inc(norm_chain[i], 1)
                wait(dve, norm_chain[i], 2 * b + 2)
                ts(var_eps[i][:, :], moments[i][:, :, 1], LN_EPS, None, ALU.add).then_inc(var_ready[i], 1)

            def moments_of(b, i):
                row_stats(b, i)
                row_moments(b, i)

            def centres(b, i):
                wait(dve, rstd_ready[i], b + 1)
                stt(centre[i][:, :], moments[i][:, :, 0], -1.0, rstd[i][:, :], ALU.mult,
                        ALU.mult).then_inc(centre_ready[i], 1)

            def normalise(b, i, half=None):
                src, dst = ln_source(b, i), (tile_of(one(b)), tile_of(x2N), tile_of(x3N))[i]
                wait(dve, rstd_ready[i], b + 1)
                if i == 1:
                    wait(dve, x3pre_ready, b)
                if i == 2:
                    wait(dve, x4pre_ready, b + 1)
                for t in range(NT) if half is None else (2 * half, 2 * half + 1):
                    last = ts(dst(t), src(t), moments[i][:, t, 0:1], rstd[i][:, t:t + 1], ALU.subtract,
                            ALU.mult)
                if half != 0:
                    last.then_inc(norm_done[i], 1)

            def mask_part(slot):
                tile = mask[:, bass.ds(slot.step, 1), :].rearrange("p a n -> p (a n)")
                diagonal = mask[:, :, :].rearrange("p t n -> p (t n)")[:, bass.ds(slot.step * (N + P), P)]
                if slot.s == 0:
                    dve.wait_ge(adjN_loaded, 16)
                    cp(tile,
                            edge[:, bass.ds(slot.step, 1), :].rearrange("p a n -> p (a n)")).then_inc(mask_step, 1)
                if slot.s == 1:
                    dve.wait_ge(mask_step, slot.step * 3 + 1)
                    tt(diagonal, diagonal, ident, ALU.add).then_inc(mask_step, 1)
                if slot.s == 2:
                    dve.wait_ge(mask_step, slot.step * 3 + 2)
                    ts(tile, tile, 0.0, MASKED, ALU.is_le, ALU.mult).then_inc(mask_step, 1)

            def norm_part(slot):
                b = slot.group * S - S + slot.step
                if slot.s == 0:
                    row_stats(b, 0)
                if slot.s == 1:
                    row_moments(b, 0)
                if slot.s >= 2:
                    normalise(b, 0, half=slot.s - 2)

            def beside(slot):
                if slot.final and slot.s == 1:
                    moments_of(B - S, 0)
                if slot.final and slot.s == 2:
                    normalise(B - S, 0)
                if not slot.last and not isinstance(slot.step, int):
                    if isinstance(slot.group, int) and slot.group == 0:
                        mask_part(slot)
                    else:
                        norm_part(slot)

            def state_low(slot):
                i = slot.i
                wait(dve, state_loaded[slot.s], 16 * slot.group + 16)
                wait(dve, h_hi_ready, slot.q + 1)
                rest(hT_lo[:, i], hT[slot.s], hT_hi[:, i]).then_inc(h_lo_ready, 1)

            def message_low(slot):
                i = slot.i
                wait(dve, m_hi_ready, slot.q + 1)
                rest(mT_lo[:, i], ps_m[i][:, :], mT_hi[:, i]).then_inc(m_lo_ready, 1)

            def reset(slot):
                i = slot.i
                wait(dve, tr_ready, slot.q + 1)
                stt(rh[:, i], tr[:, i], 1.0, hT[slot.s], ALU.add, ALU.mult).then_inc(rh_ready, 1)

            def reset_low(slot):
                i = slot.i
                wait(dve, rh_hi_ready, slot.q + 1)
                rest(rh_lo[:, i], rh[:, i], rh_hi[:, i]).then_inc(rh_lo_ready, 1)

            def update_1(slot):
                i = slot.i
                wait(dve, th_ready, slot.q + 1)
                tt(dh[:, i], th[:, i], hT[slot.s], ALU.subtract).then_inc(dh_ready, 1)

            def update_2(slot):
                i = slot.i
                wait(dve, dh_ready, slot.q + 1)
                stt(dh[:, i], tz[:, i], 1.0, dh[:, i], ALU.add, ALU.mult).then_inc(step_ready, 1)

            def update_3(slot):
                i = slot.i
                wait(dve, step_ready, slot.q + 1)
                stt(hT[slot.s], dh[:, i], 0.5, hT[slot.s], ALU.mult, ALU.add).then_inc(h_ready, 1)

            def natural_low(slot):
                i = slot.i
                wait(dve, h_turned, slot.q + 1)
                if not slot.last:
                    wait(dve, hN_hi_ready, S + slot.q + 1)
                    rest(hN[:, slot.s, 1], tiles(ps_t[i]), hN[:, slot.s, 0]).then_inc(hN_lo_ready, 1)
                    return
                dve.wait_ge(x_rest_loaded, 16 * (GROUPS - 1))
                done = tt(slot.graph(), slot.graph(), tiles(ps_t[i]), ALU.add)
                if not slot.final:
                    wait(dve, hN_hi_ready, S + slot.q + 1)
                    done = rest(hN[:, slot.s, 1], slot.graph(S), hN[:, slot.s, 0])
                done.then_inc(hN_lo_ready, 1)

            slots(dve, ((message_low, 2), (reset, 1), (update_3, 0), (reset_low, 1), (state_low, 3),
                        (natural_low, 0), (beside, 0), (update_1, 1), (update_2, 1)))

            def scores(b):
                wait(dve, near_ready, b + 1)
                carry(5)
                for t in range(NT):
                    last = nc.vector.tensor_tensor_reduce(state[:, t, :], A2[:, :], mask[:, t, :], 1.0, MASKED,
                                                          ALU.add, ALU.max, row_max[:, t:t + 1])
                last.then_inc(scores_ready, 1)

            def own_terms(b):
                wait(dve, x1_moved, 16 * b + 16)
                wait(dve, shifts_ready, b)
                carry(10)
                for t in range(NT):
                    last = nc.vector.tensor_tensor_reduce(product[:, 0, t, :], x1N[:, t, :],
                            wa_src_row[:, :], 1.0, 0.0,
                                                          ALU.mult, ALU.add, own[:, t:t + 1])
                last.then_inc(own_ready, 1)

            def shifts(b):
                c = Chain(dve, shift_chain, 3, b)
                wait(dve, scores_ready, b + 1)
                wait(dve, own_ready, b + 1)
                c.link(tt(s_max[:, :], own[:, :], row_max[:, :], ALU.add))
                c.link(ts(s_leak[:, :], s_max[:, :], SLOPE, None, ALU.mult))
                c.link(tt(shift[:, :], s_max[:, :], s_leak[:, :], ALU.max))
                c.close()
                tt(bias_1[:, :], own[:, :], shift[:, :], ALU.subtract)
                stt(bias_s[:, :], own[:, :], SLOPE, shift[:, :], ALU.mult,
                        ALU.subtract).then_inc(shifts_ready, 1)

            def probabilities(b, t):
                wait(dve, exps_ready, b * NT + t + 1)
                stt(prob[:, t, :], e_hi[:, t % 2], 1.0, e_lo[:, t % 2], ALU.mult, ALU.max,
                    accum_out=row_sum[:, t:t + 1]).then_inc(probs_ready, 1)

            def row_inverse(b):
                wait(dve, probs_ready, b * NT + NT)
                nc.vector.reciprocal(row_inv[:, :], row_sum[:, :]).then_inc(row_inv_ready, 1)

            def last_group(b, part):
                if not (isinstance(b, int) and b == 0):
                    return
                step, graph = ((moments_of, B - 3), (normalise, B - 3), (row_stats, B - 2),
                        (row_moments, B - 2),
                               (normalise, B - 2), (moments_of, B - 1), (normalise, B - 1))[part]
                step(graph, 0)

            def elu_residual(b):
                wait(dve, elu_exp_ready, b + 1)
                wait(dve, elu_relu_ready, b + 1)
                wait(dve, norm_done[1], b)
                stt(rl[:, :, :], ex[:, :, :], 1.0, rl[:, :, :], ALU.min, ALU.add).then_inc(elu_ready, 1)
                wait(dve, elu_ready, b + 1)
                stt(x2pre[:, :, :], rl[:, :, :], -1.0, one(b), ALU.add, ALU.add).then_inc(x2pre_ready, 1)

            def y_residual(b):
                wait(dve, y_ready, b + 1)
                wait(dve, norm_done[2], b)
                for q, psum in enumerate((B2, B0)):
                    two = slice(2 * q, 2 * q + 2)
                    last = tt(x3pre[:, two, :],
                            psum[:, :].rearrange("p (t k d) -> p t k d", t=2, k=2)[:, :, 1, :],
                              x2N[:, two, :], ALU.add)
                last.then_inc(x3pre_ready, 1)

            def pair_moments(b):
                wait(dve, pq_ready, b + 1)
                nc.vector.bn_stats(e_stats[:, :], C0[:, :]).then_inc(pair_stats_ready, 1)
                wait(dve, pair_stats_ready, b + 1)
                carry(4)
                nc.vector.bn_aggr(e_mom[:, :], e_stats[:, :]).then_inc(pair_moments_ready, 1)

            def pair_variance(b):
                wait(dve, pair_sums_ready, b + 1)
                cp(e_mean[:, :], C0[:, 0:1])
                ts(e_var[:, :], C0[:, 1:2], EDGE_EPS, None, ALU.add).then_inc(pair_var_ready, 1)

            def q_terms(b):
                wait(dve, norm_done[2], b + 1)
                wait(dve, columns_ready, b)
                carry(11)
                for t in range(NT):
                    last = nc.vector.tensor_tensor_reduce(product[:, 1, t, :], x3N[:, t, :],
                            a_j_row[:, :], 1.0, 0.0,
                                                          ALU.mult, ALU.add, q_cols[:, t:t + 1])
                last.then_inc(q_cols_ready, 1)

            def column_terms(b):
                c = Chain(dve, columns_chain, 1, b)
                wait(dve, pair_rstd_ready, b + 1)
                wait(dve, q_cols_ready, b + 1)
                c.link(ts(c_norm[:, :], q_cols[:, :], e_mean[:, :], e_rstd[:, :], ALU.subtract, ALU.mult))
                c.close()
                ts(c_one[:, :], c_norm[:, :], 1.0, None, ALU.add).then_inc(columns_ready, 1)

            def edge_scores(b, j):
                wait(dve, normed_ready, b * NT + j + 1)
                carry(6 + j)
                nc.vector.tensor_tensor_reduce(edge[:, j, :], scaled[:, j % 2], adjT[:, j, :], 1.0, -3.0e38,
                                               ALU.mult, ALU.max, col_max[:,
                                                       j:j + 1]).then_inc(edge_scores_ready, 1)

            def column_shifts(b):
                c = Chain(dve, maxima_chain, 1, b)
                wait(dve, edge_scores_ready, b * NT + NT)
                c.link(ts(col_neg[:, :], col_max[:, :], -1.0, None, ALU.mult))
                c.close()
                stt(col_shift[:, :], col_max[:, :], -SLOPE, col_neg[:, :], ALU.mult,
                        ALU.min).then_inc(column_shift_ready, 1)

            def leaky(b, j):
                wait(dve, edge_scores_ready, b * NT + j + 1)
                stt(edge[:, j, :], edge[:, j, :], SLOPE, edge[:, j, :], ALU.mult,
                        ALU.max).then_inc(leaky_ready, 1)

            def column_inverse(b):
                wait(dve, edge_exps_ready, b * NT + NT)
                nc.vector.reciprocal(col_inv[:, :], col_sum[:, :]).then_inc(column_inv_ready, 1)

            def sigmoid_residual(b):
                wait(dve, sigmoid_ready, b + 1)
                wait(dve, norm_done[3], b)
                tt(x4pre[:, :, :], sgN[:, :, :], x3N[:, :, :], ALU.add).then_inc(x4pre_ready, 1)

            ticks(dve, ((own_terms, 0), (last_group, 0, 0), (column_inverse, 4), (y_residual, 3),
                   (moments_of, 3, 2), (normalise, 2, 1), (scores, 0), (shifts, 0), (last_group, 0, 1),
                   (sigmoid_residual, 4), (normalise, 3, 2), (probabilities, 0, 0), (last_group, 0, 2),
                   (q_terms, 3), (probabilities, 0, 1), (last_group, 0, 3), (moments_of, 4, 3),
                   (pair_moments, 3), (probabilities, 0, 2), (pair_variance, 3), (probabilities, 0, 3),
                   (last_group, 0, 4), (column_terms, 3), (last_group, 1, 6), (elu_residual, 1),
                   (edge_scores, 3, 0), (edge_scores, 3, 1), (centres, 4, 3), (row_inverse, 0),
                   (last_group, 0, 5), (edge_scores, 3, 2), (edge_scores, 3, 3), (leaky, 3, 0),
                   (column_shifts, 3), (leaky, 3, 1), (leaky, 3, 2), (leaky, 3, 3), (moments_of, 1, 1)))

        @block.gpsimd
        def _(pool):
            pool.wait_ge(x4pre_ready, 1)

            def root(b, i):
                wait(pool, var_ready[i], b + 1)
                nc.gpsimd.tensor_tensor(rstd[i][:, :], var_eps[i][:, :], minus_half[:, :],
                        ALU.pow).then_inc(rstd_ready[i], 1)

            def pair_root(b):
                wait(pool, pair_var_ready, b + 1)
                nc.gpsimd.tensor_tensor(e_rstd[:, :], e_var[:, :], minus_half[:, 0:1],
                        ALU.pow).then_inc(pair_rstd_ready, 1)

            def x2_low(b):
                wait(pool, x2_hi_ready, b + 1)
                nc.gpsimd.tensor_tensor(x2N_lo, x2N[:, :, :], x2N_hi.bitcast(F32),
                        ALU.subtract).then_inc(x2_lo_ready, 1)

            with pool.Fori(0, B, 1) as b:
                root(b, 0)

            ticks(pool, ((root, 3, 2), (x2_low, 2), (pair_root, 3), (root, 4, 3), (root, 1, 1)))


def kernel(x, adj, L0_gnn_w3_w, L0_gnn_w3_b, L0_gnn_u3_w, L0_gnn_u3_b, L0_gnn_w4_w, L0_gnn_w4_b, L0_gnn_w5_w,
           L0_gnn_w5_b, L0_gnn_u5_w, L0_gnn_u5_b, L1_gnn_W, L1_gnn_a_src, L1_gnn_a_dst, L2_gnn_weight_1, L3_gnn_a):
    import numpy as np
    import concourse.bacc as bacc
    from concourse.bass_utils import run_bass_kernel_spmd

    x = np.asarray(x)
    B, N, D = x.shape
    NT = N // P

    def nodes_first(a):
        return np.asarray(a).reshape(NT, P, -1).transpose(1, 0, 2)

    def halves(a):
        return np.asarray(a).reshape(D, 2, D).transpose(2, 1, 0).reshape(D, 2 * D)

    def col(a):
        return np.asarray(a).reshape(D, -1)

    a = np.asarray(L3_gnn_a)
    keep = dict(u3T=np.asarray(L0_gnn_u3_w).T, w_gat=np.asarray(L1_gnn_W), ident=np.eye(P, dtype=np.float32),
                a_src=col(L1_gnn_a_src), a_dst=col(L1_gnn_a_dst), a_i=a[:D], a_j=a[D:], w3_b=col(L0_gnn_w3_b),
                u3_b=col(L0_gnn_u3_b), w4_b=col(L0_gnn_w4_b), w5_b=col(L0_gnn_w5_b), u5_b=col(L0_gnn_u5_b),
                u5T=np.asarray(L0_gnn_u5_w).T)
    temp = dict(w3T=halves(L0_gnn_w3_w), w4T=halves(L0_gnn_w4_w), w5T=halves(L0_gnn_w5_w),
                cheb=np.asarray(L2_gnn_weight_1).transpose(0, 2, 1).reshape(D,
                        -1), w_gatT=np.asarray(L1_gnn_W).T)
    arrays = dict(
        x_nat=x.reshape(B, NT, P, D).transpose(2, 0, 1, 3),
        x_tr=x.transpose(2, 0, 1),
        adj_nat=nodes_first(adj),
        adj_tr=nodes_first(np.asarray(adj).T),
        keep_pack=np.concatenate([keep[n] for n in KEEP], axis=1),
        temp_pack=np.concatenate([temp[n] for n in TEMP], axis=1),
    )
    arrays = {n: np.ascontiguousarray(v) for n, v in arrays.items()}
    nc = bacc.Bacc("TRN2", target_bir_lowering=False, num_devices=1)
    aps = {n: nc.dram_tensor(n, v.shape, F32, kind="ExternalInput").ap() for n, v in arrays.items()}
    aps["out"] = nc.dram_tensor("out", (P, B, NT, D), F32, kind="ExternalOutput").ap()
    build(nc, **aps)
    got = run_bass_kernel_spmd(nc, [arrays], core_ids=[0]).results[0]["out"]
    return np.ascontiguousarray(np.asarray(got).reshape(P, B, NT, D).transpose(1, 2, 0, 3).reshape(B, N, D))
```
